# Optimizing a Trainium2 kernel written in Bass

```python
import numpy as np
import jax
import jax.numpy as jnp

def _softmax(x, axis=-1):
    return jax.nn.softmax(x, axis=axis)

def _gelu(x):
    return jax.nn.gelu(x, approximate=True)

def _silu(x):
    return jax.nn.silu(x)

def _sigmoid(x):
    return jax.nn.sigmoid(x)

def _layernorm(x, axis=-1, eps=1e-05):
    m = jnp.mean(x, axis=axis, keepdims=True)
    v = jnp.var(x, axis=axis, keepdims=True)
    return (x - m) / jnp.sqrt(v + eps)

def _scatter_add(tgt, idx, src, axis=0):
    return tgt.at[idx].add(src)

def _segment_sum(src, seg, n):
    return jax.ops.segment_sum(src, seg, n)
kernel_name = 'mk_xattn_seq_d2_seqx_r4_71c1c6'

def setup_inputs(seed: int=0):
    np.random.seed(seed)
    _w = jnp.asarray

    def _rec_inputs():
        import jax
        import jax.numpy as jnp
        _rk = jax.random.key(seed)
        x = -0.0002928 + 1 * jax.random.normal(jax.random.fold_in(_rk, 1), (16, 256, 512), jnp.float32)
        _lenS = 256 - jax.random.randint(jax.random.fold_in(_rk, 7), (16,), 0, max(1, 256 // 4) + 1, jnp.int32)
        _lenS2 = 256 - jax.random.randint(jax.random.fold_in(_rk, 8), (16,), 0, max(1, 256 // 4) + 1, jnp.int32)
        _ctx_2048P = jax.random.normal(jax.random.fold_in(_rk, 12), (16, 16, 512), jnp.float32)
        _ctx_2048c = jax.random.dirichlet(jax.random.fold_in(_rk, 512), 0.3 * jnp.ones((16,), jnp.float32), (16, 256))
        _ctx_2048t = jnp.einsum('bsk,bkd->bsd', _ctx_2048c, _ctx_2048P)
        _ctx_2048t = _ctx_2048t * jax.lax.rsqrt(jnp.mean(jnp.square(_ctx_2048t)) + 1e-12) * 0.953939
        ctx_2048 = -1.39393e-06 + 0.999914 * (_ctx_2048t + 0.3 * jax.random.normal(jax.random.fold_in(_rk, 612), (16, 256, 512), jnp.float32))
        _validS = jnp.arange(256)[None, :] < _lenS[:, None]
        _validS2 = jnp.arange(256)[None, :] < _lenS2[:, None]
        _causal = jnp.tril(jnp.ones((256, 256), dtype=bool))
        mask_Bx1x2048_bf1 = jnp.ones((16, 1, 512), dtype=bool)
        return (x, ctx_2048, mask_Bx1x2048_bf1)
    x, ctx_2048, mask_Bx1x2048_bf1 = _rec_inputs()

    def _L0_xattn_setup():
        import jax, jax.numpy as jnp
        import numpy as np
        import math
        N_HEADS = 16
        EPS = 1e-05

        def _masked_instance_norm(x, mask):
            m = mask.astype(x.dtype)
            x = x * m
            n_valid = jnp.sum(m, axis=-1, keepdims=True)
            mean = jnp.sum(x, axis=-1, keepdims=True) / n_valid
            var = jnp.sum(x * x, axis=-1, keepdims=True) / n_valid - mean * mean
            x = (x - mean) / jnp.sqrt(jax.nn.relu(var) + EPS)
            return x * m
        key = jax.random.key(seed)
        ks = jax.random.split(key, 8)
        bs, c, t1, t2 = (2, 256, 512, 512)
        s = 1.0 / math.sqrt(c)
        return {'x': jax.random.normal(ks[0], (bs, c, t1), jnp.float32), 'mask': jnp.ones((bs, 1, t1), jnp.bool_), 'kv': jax.random.normal(ks[1], (bs, c, t2), jnp.float32), 'kv_mask': jnp.ones((bs, 1, t2), jnp.bool_), 'Wq': jax.random.normal(ks[2], (c, c), jnp.float32) * s, 'bq': jnp.zeros((c,), jnp.float32), 'Wk': jax.random.normal(ks[3], (c, c), jnp.float32) * s, 'bk': jnp.zeros((c,), jnp.float32), 'Wv': jax.random.normal(ks[4], (c, c), jnp.float32) * s, 'bv': jnp.zeros((c,), jnp.float32)}
    _L0_xattn_all = _L0_xattn_setup()
    _L0_xattn_in = {k: v for k, v in _L0_xattn_all.items() if k in ('Wq', 'bq', 'Wk', 'bk', 'Wv', 'bv')}
    del _L0_xattn_all

    def _L1_xattn_setup():
        import jax, jax.numpy as jnp
        import numpy as np
        B, C1, C2, N = (8, 256, 256, 512)
        D = C2 // 8
        key = jax.random.key(seed)
        ks = jax.random.split(key, 8)
        s1 = 1.0 / np.sqrt(C1)
        s2 = 1.0 / np.sqrt(C2)
        return {'x1': jax.random.normal(ks[0], (B, C1, N), jnp.float32), 'x2': jax.random.normal(ks[1], (B, C2, N), jnp.float32), 'Wq': jax.random.uniform(ks[2], (D, C1), jnp.float32, -s1, s1), 'bq': jax.random.uniform(ks[3], (D,), jnp.float32, -s1, s1), 'Wk': jax.random.uniform(ks[4], (D, C2), jnp.float32, -s2, s2), 'bk': jax.random.uniform(ks[5], (D,), jnp.float32, -s2, s2), 'Wv': jax.random.uniform(ks[6], (C1, C2), jnp.float32, -s2, s2), 'bv': jax.random.uniform(ks[7], (C1,), jnp.float32, -s2, s2)}
    _L1_xattn_all = _L1_xattn_setup()
    _L1_xattn_in = {k: v for k, v in _L1_xattn_all.items() if k in ('Wq', 'bq', 'Wk', 'bk', 'Wv', 'bv')}
    del _L1_xattn_all
    return {'x': x, 'ctx_2048': ctx_2048, 'mask_Bx1x2048_bf1': mask_Bx1x2048_bf1, 'L0_xattn_Wq': _L0_xattn_in['Wq'], 'L0_xattn_bq': _L0_xattn_in['bq'], 'L0_xattn_Wk': _L0_xattn_in['Wk'], 'L0_xattn_bk': _L0_xattn_in['bk'], 'L0_xattn_Wv': _L0_xattn_in['Wv'], 'L0_xattn_bv': _L0_xattn_in['bv'], 'L1_xattn_Wq': _L1_xattn_in['Wq'], 'L1_xattn_bq': _L1_xattn_in['bq'], 'L1_xattn_Wk': _L1_xattn_in['Wk'], 'L1_xattn_bk': _L1_xattn_in['bk'], 'L1_xattn_Wv': _L1_xattn_in['Wv'], 'L1_xattn_bv': _L1_xattn_in['bv']}

def reference(x, ctx_2048, mask_Bx1x2048_bf1, L0_xattn_Wq, L0_xattn_bq, L0_xattn_Wk, L0_xattn_bk, L0_xattn_Wv, L0_xattn_bv, L1_xattn_Wq, L1_xattn_bq, L1_xattn_Wk, L1_xattn_bk, L1_xattn_Wv, L1_xattn_bv):
    import jax
    import jax.numpy as jnp

    def _L0_xattn_ref(x, mask, kv, kv_mask, Wq, bq, Wk, bk, Wv, bv):
        import jax, jax.numpy as jnp
        import numpy as np
        import math
        N_HEADS = 16
        EPS = 1e-05

        def _masked_instance_norm(x, mask):
            m = mask.astype(x.dtype)
            x = x * m
            n_valid = jnp.sum(m, axis=-1, keepdims=True)
            mean = jnp.sum(x, axis=-1, keepdims=True) / n_valid
            var = jnp.sum(x * x, axis=-1, keepdims=True) / n_valid - mean * mean
            x = (x - mean) / jnp.sqrt(jax.nn.relu(var) + EPS)
            return x * m
        bs, c, t1 = x.shape
        h = N_HEADS
        d = c // h
        scale = 1.0 / math.sqrt(d)
        q = jnp.einsum('oc,bct->bot', Wq, x) + bq[None, :, None]
        k = jnp.einsum('oc,bct->bot', Wk, kv) + bk[None, :, None]
        v = jnp.einsum('oc,bct->bot', Wv, kv) + bv[None, :, None]
        q = q.reshape(bs, h, d, t1).transpose(0, 1, 3, 2)
        k = k.reshape(bs, h, d, -1)
        v = v.reshape(bs, h, d, -1).transpose(0, 1, 3, 2)
        attn = jnp.einsum('bhqd,bhdk->bhqk', q * scale, k)
        attn = jnp.where(kv_mask[:, :, None, :], attn, -jnp.inf)
        attn = jax.nn.softmax(attn, axis=-1)
        mean = jnp.einsum('bhqk,bhkd->bhqd', attn, v)
        ex2 = jnp.einsum('bhqk,bhkd->bhqd', attn, v * v)
        std = jnp.sqrt(jax.nn.relu(ex2 - mean * mean))
        mean = mean.transpose(0, 1, 3, 2).reshape(bs, c, t1)
        std = std.transpose(0, 1, 3, 2).reshape(bs, c, t1)
        xn = _masked_instance_norm(x, mask)
        out = (xn * std + mean) * mask.astype(x.dtype)
        return out

    def _L1_xattn_ref(x1, x2, Wq, bq, Wk, bk, Wv, bv):
        import jax, jax.numpy as jnp
        import numpy as np
        B, C1, C2, N = (8, 256, 256, 512)
        D = C2 // 8
        q = jnp.einsum('bcn,dc->bnd', x1, Wq) + bq
        k = jnp.einsum('bcn,dc->bdn', x2, Wk) + bk[:, None]
        v = jnp.einsum('bcn,dc->bdn', x2, Wv) + bv[:, None]
        attn = jax.nn.softmax(jnp.einsum('bnd,bdm->bnm', q, k), axis=2)
        attn_out = jnp.einsum('bcm,bnm->bcn', v, attn)
        return attn_out + x1
    x = _L0_xattn_ref(x, mask_Bx1x2048_bf1, ctx_2048, mask_Bx1x2048_bf1, L0_xattn_Wq, L0_xattn_bq, L0_xattn_Wk, L0_xattn_bk, L0_xattn_Wv, L0_xattn_bv)
    x = _L1_xattn_ref(x, ctx_2048, L1_xattn_Wq, L1_xattn_bq, L1_xattn_Wk, L1_xattn_bk, L1_xattn_Wv, L1_xattn_bv)
    return x

_drawn_inputs = setup_inputs


def setup_inputs(seed=0):
    import zlib

    import numpy as np

    out = dict(_drawn_inputs(seed))
    spreads = {'L0_xattn_bq': (0.0, 0.1), 'L0_xattn_bk': (0.0, 0.1), 'L0_xattn_bv': (0.0, 0.1)}
    factors = {}
    for name, (base, spread) in spreads.items():
        noise = np.random.default_rng([zlib.crc32(name.encode()), seed]).standard_normal(out[name].shape)
        drawn = base * np.exp(spread * noise) if base else spread * noise
        out[name] = jnp.asarray(drawn.astype(out[name].dtype))
    for name, factor in factors.items():
        out[name] = (out[name] * factor).astype(out[name].dtype)
    return out
```

```python
import concourse.bass as bass
from concourse import mybir
from contextlib import ExitStack

B, C, T = 16, 256, 512
HEADS, D = 16, 16
D1 = 32
P = 128
CH = C // P
KB = T // P
HALF = HEADS // 2
STEPS = 2 * HEADS
GROUP = 4
SUBS = STEPS // GROUP
PARTS = 3
Q_PARTS = (0, 1, 0, 1, 0, 2)
K_PARTS = (0, 0, 1, 1, 2, 0)
ROW_MASK = D * len(Q_PARTS)
ROW_MAX = ROW_MASK + 1
ROWS = ROW_MAX + PARTS
SCALE = 1.0 / float(D) ** 0.5
MASKED = 3.0e38
TWO_BF16_ONES = 1.0 + 0x3F80 * 2.0 ** -23
EPS = 1e-5
RING = 3

FILLERS = {
    1: [("shift", 0, 1), ("q", 2, 0)],
    5: [("k", 2, 0)],
    9: [("v", 1, 0)],
    13: [("k2", -1, 0)],
    17: [("shift", 1, 0), ("v2", -1, 0)],
    18: [("q2", -1, 0)],
    21: [("s2", -1, 0), ("s2", -1, 1)],
    25: [("t2", -1, 0), ("t2", -1, 1)],
    29: [("o2", -1, 0), ("o2", -1, 1)],
}
JOBS = []
for _t in range(STEPS):
    JOBS += [("st", 0, _t), ("mx", 1, _t)] + FILLERS.get(_t, [])
assert len(JOBS) % RING == 0
assert all(kind in ("st", "mx") for kind, _, _ in JOBS[-RING:])
FIRST, LAST = -2, B
LOOP_FROM, LOOP_TO = 1, B - 3

LOOP_I = 8


class Looped:

    def __init__(self, i, c):
        self.i, self.c = i, c

    def __add__(self, n):
        return Looped(self.i, self.c + n)

    def __sub__(self, n):
        return Looped(self.i, self.c - n)

    def times(self, per, n):
        return self.i * (2 * per) + (self.c * per + n)


def index(d):
    return d if isinstance(d, int) else d.times(1, 0)


def exists(d):
    return not isinstance(d, int) or 0 <= d < B


def ring_place(kind, off, n):
    return JOBS.index((kind, off, n)) % RING


def ring_before(b, kind, off, n):
    at = JOBS.index((kind, off, n))
    back = 0
    while True:
        at -= RING
        if at < 0:
            at += len(JOBS)
            back += 1
        k, o, m = JOBS[at]
        d = b - back + o
        if isinstance(b, int) and b - back < FIRST:
            return None
        if exists(d):
            return k, d, m


def build(nc, x_in, ctx_in, mask_in, wqT, bq, wkT, bk, wvT, bv, w1qT, b1q, w1kT, b1k, w1vT, b1v, out):
    fp32, bf16, fp32r = mybir.dt.float32, mybir.dt.bfloat16, mybir.dt.float32r
    ALU, ACT, AX = mybir.AluOpType, mybir.ActivationFunctionType, mybir.AxisListType

    parts_dram = [[nc.dram_tensor(f"parts_{n}{p}", (PARTS, C, T), bf16, kind="Internal").ap()
                   for p in range(2)] for n in "qk"]
    shift_dram = [[nc.dram_tensor(f"shift_{h}{p}", (PARTS, HALF * KB, P), bf16, kind="Internal").ap()
                   for p in range(2)] for h in range(2)]
    maskrow_dram = nc.dram_tensor("maskrow", (B, HEADS * T), bf16, kind="Internal").ap()

    ctx = ExitStack()
    with ctx:
        def sb(name, shape, dt):
            return ctx.enter_context(nc.sbuf_tensor(name, shape, dt))

        def sem(name):
            return ctx.enter_context(nc.semaphore(name))

        class Tally:

            def __init__(self, name, per):
                self.sem, self.per = sem(name), per

            def after(self, d, n):
                return self.sem, (max(d * self.per + n, 0) if isinstance(d, int) else d.times(self.per, n))

        turns = sem("turns")

        wq_sb, wk_sb = sb("wq_sb", [P, CH, C], fp32), sb("wk_sb", [P, CH, C], fp32)
        wv_sb, w1v_sb = sb("wv_sb", [P, CH, C], fp32), sb("w1v_sb", [P, CH, C], fp32)
        w1q_sb, w1k_sb = sb("w1q_sb", [P, CH, P], fp32), sb("w1k_sb", [P, CH, P], fp32)
        bq_sb, bk_sb = sb("bq_sb", [P, CH], fp32), sb("bk_sb", [P, CH], fp32)
        b1q_sb, b1k_sb = sb("b1q_sb", [P, 1], fp32), sb("b1k_sb", [P, 1], fp32)
        bv_sb, b1v_sb = sb("bv_sb", [P, C], fp32), sb("b1v_sb", [P, C], fp32)
        ident, ones = sb("ident", [P, P], fp32), sb("ones", [P, 32], fp32)
        mask_u8 = sb("mask_u8", [B, T], mybir.dt.uint8)
        xs, ctx_k = sb("xs", [P, CH, T], fp32), sb("ctx_k", [P, CH, T], fp32)
        ctx_v = sb("ctx_v", [P, CH, T], fp32)
        split, rest = sb("split", [P, CH, PARTS, T], bf16), sb("rest", [P, T], fp32)
        q_stack = [sb(f"q_stack{p}", [P, HEADS, T], bf16) for p in range(2)]
        k_stack = [sb(f"k_stack{p}", [P, HEADS, T], bf16) for p in range(2)]
        row_max = sb("row_max", [P, 2, HALF * KB], fp32)
        neg_max, neg_rest = sb("neg_max", [32, PARTS, P], bf16), sb("neg_rest", [32, P], fp32)
        values = [sb(f"values{p}", [P, KB, HEADS, 2 * D], fp32) for p in range(2)]
        probs = [sb(f"probs{p}", [P, GROUP, 2, T], fp32) for p in range(2)]
        pairs = [sb(f"pairs{p}", [P, GROUP, T], fp32) for p in range(2)]
        recip, normed = sb("recip", [P, T], fp32), [sb(f"normed{p}", [P, T], fp32) for p in range(2)]
        mean, ex2 = sb("mean", [P, CH, T], fp32), sb("ex2", [P, CH, T], fp32)
        mask_b8, mask_b = sb("mask_b8", [P, T], mybir.dt.uint8), sb("mask_b", [P, T], fp32)
        stats, spread = sb("stats", [P, 16], fp32), sb("spread", [P, CH], fp32)
        x1 = sb("x1", [P, CH, T], fp32)
        q2, k2 = sb("q2", [P, T], fp32r), sb("k2", [P, T], fp32r)
        values2 = sb("values2", [P, KB, C], fp32)
        probs2, probs2T = sb("probs2", [P, KB, T], fp32), sb("probs2T", [P, KB, T], fp32)
        stats2 = sb("stats2", [P, 3, KB], fp32)
        mask_f = probs[1][0:B, 0, 0, :]
        maskrow = probs[0][0:B, :, :, :].rearrange("p a b t -> p (a b t)").bitcast(bf16)[:, 0:HEADS * T]
        square = probs2T
        junk = recip

        ring = ctx.enter_context(nc.psum_tensor("ring", [P, RING, 2, T], fp32))
        att = ctx.enter_context(nc.psum_tensor("att", [P, T], fp32))
        den = ctx.enter_context(nc.psum_tensor("den", [P, T], fp32))

        weights_in, consts, ones_made, mask_scaled = sem("weights_in"), sem("consts"), sem("ones_made"), sem("mask_scaled")
        maskrow_made, maskrow_out = sem("maskrow_made"), sem("maskrow_out")
        xq_in, xr_in = Tally("xq_in", 16), Tally("xr_in", 16)
        ctxk_in, ctxv_in, ctx1_in = Tally("ctxk_in", 16), Tally("ctxv_in", 16), Tally("ctx1_in", 16)
        mask_in_ = Tally("mask_in_", 16)
        parts_out = [Tally(f"parts_out_{n}", 32) for n in "qk"]
        stack_in = [Tally(f"stack_in{h}", 16 * 2 * len(Q_PARTS)) for h in range(2)]
        maskrow_in = [Tally(f"maskrow_in{h}", 16) for h in range(2)]
        shift_out = [Tally(f"shift_out{h}", 16) for h in range(2)]
        shift_in = [Tally(f"shift_in{h}", 16) for h in range(2)]
        moments_in = [Tally(f"moments_in{n}", 16 * HEADS) for n in range(2)]
        result_out = Tally("result_out", 16)
        made = {k: Tally(f"made_{k}", n) for k, n in dict(
            st=STEPS, mx=STEPS, q=1, k=1, v=1, shift=2, k2=1, v2=1, q2=1, s2=2, t2=2, o2=2).items()}
        att_done, den_done = Tally("att_done", SUBS), Tally("den_done", SUBS)
        exp_done, max_done = Tally("exp_done", STEPS), Tally("max_done", STEPS)
        rest_made = [Tally(f"rest_made_{n}", 2) for n in "qk"]
        v_biased, shift_rest = Tally("v_biased", 1), Tally("shift_rest", 2)
        k2_made, v2_made, q2_made = Tally("k2_made", 1), Tally("v2_made", 1), Tally("q2_made", 1)
        exp2_done, probs2T_made, result_made = Tally("exp2_done", KB), Tally("probs2T_made", 2), Tally("result_made", 2)
        FREED = dict(st=(exp_done, 1), mx=(max_done, 1), q=(rest_made[0], 2), k=(rest_made[1], 2),
                     v=(v_biased, 1), shift=(shift_rest, 1), k2=(k2_made, 1), v2=(v2_made, 1),
                     q2=(q2_made, 1), s2=(exp2_done, 2), t2=(probs2T_made, 1), o2=(result_made, 1))
        part1 = [Tally(f"part1_{n}", 2) for n in "qk"]
        part2 = [Tally(f"part2_{n}", 2) for n in "qk"]
        part3 = [Tally(f"part3_{n}", 2) for n in "qk"]
        neg1, neg2, neg3 = Tally("neg1", 2), Tally("neg2", 2), Tally("neg3", 2)
        v_squared, pair_done = Tally("v_squared", 1), Tally("pair_done", STEPS)
        recip_done, normed_done = Tally("recip_done", 4), Tally("normed_done", 4)
        mask_ready, x_masked = Tally("mask_ready", 1), Tally("x_masked", 1)
        n_valid, x_sum, x_sumsq = Tally("n_valid", 1), Tally("x_sum", 1), Tally("x_sumsq", 2)
        stat_steps = Tally("stat_steps", 7)
        spread_done, std_done = Tally("spread_done", 1), Tally("std_done", 1)
        mean_squared, var_made, var_clamped = Tally("mean_squared", 1), Tally("var_made", 1), Tally("var_clamped", 1)
        x_centred, x_styled, x_shifted, x1_made = (Tally("x_centred", 2), Tally("x_styled", 2),
                                                   Tally("x_shifted", 1), Tally("x1_made", 1))
        q2_hi, k2_hi = Tally("q2_hi", 1), Tally("k2_hi", 2)
        max2_done, sum2_inv, probs2_made = Tally("max2_done", 2), Tally("sum2_inv", 1), Tally("probs2_made", 1)

        def slot(kind, off, n):
            return ring[:, ring_place(kind, off, n)]

        def iterations(eng, body):
            for b in range(FIRST, LOOP_FROM):
                body(b, b % 2)
            with eng.Fori(LOOP_I, LOOP_I + (LOOP_TO - LOOP_FROM) // 2) as i:
                body(Looped(i, LOOP_FROM - 2 * LOOP_I), LOOP_FROM % 2)
                body(Looped(i, LOOP_FROM + 1 - 2 * LOOP_I), (LOOP_FROM + 1) % 2)
            for b in range(LOOP_TO, LAST + 1):
                body(b, b % 2)

        block = ctx.enter_context(nc.Block())

        @block.sync
        def _(sp):
            for dst, src in ((wq_sb, wqT), (wk_sb, wkT), (wv_sb, wvT), (w1v_sb, w1vT), (w1q_sb, w1qT), (w1k_sb, w1kT)):
                sp.dma_start(dst[:, :, :], src.rearrange("(c p) o -> p c o", p=P)).then_inc(weights_in, 16)
            for dst, src in ((bq_sb, bq), (bk_sb, bk), (b1q_sb, b1q), (b1k_sb, b1k)):
                sp.dma_start(dst[:, :], src).then_inc(weights_in, 16)
            for dst, src in ((bv_sb, bv), (b1v_sb, b1v)):
                sp.dma_start(dst[:, :], src.partition_broadcast(P)).then_inc(weights_in, 16)
            sp.dma_start(mask_u8[:, :], mask_in).then_inc(weights_in, 16)
            sp.wait_ge(consts, 4)
            sp.wait_ge(ones_made, 3)
            sp.wait_ge(maskrow_made, HEADS)
            sp.dma_start(maskrow_dram, maskrow).then_inc(maskrow_out, 16)
            sp.wait_ge(maskrow_out, 16)

            def load_stack(d, p, half):
                sp.wait_ge(*made["st"].after(d - 2, 16 * half + 16))
                sp.sem_inc(turns, 1)
                sp.wait_ge(*stack_in[half].after(d, 0))
                sp.sem_inc(turns, 1)
                sp.wait_ge(*parts_out[0].after(d, 32))
                sp.sem_inc(turns, 1)
                sp.wait_ge(*parts_out[1].after(d, 32))
                here = slice(half * HALF, half * HALF + HALF)
                for n, (stack, order) in enumerate(((q_stack[p], Q_PARTS), (k_stack[p], K_PARTS))):
                    for j, part in enumerate(order):
                        src = parts_dram[n][p][part, half * P:half * P + P, :]
                        sp.dma_start(stack[D * j:D * j + D, here, :], src.rearrange("(h d) t -> d h t", d=D))\
                            .then_inc(stack_in[half].sem, 16)

            def load_shift(d, p, half):
                sp.wait_ge(*neg3.after(d, half + 1))
                sp.sem_inc(turns, 1)
                sp.wait_ge(*shift_out[half].after(d, 0))
                sp.dma_start(shift_dram[half][p].rearrange("s r i -> r s i"), neg_max[:, :, :])\
                    .then_inc(shift_out[half].sem, 16)
                sp.wait_ge(*shift_out[half].after(d, 16))
                sp.sem_inc(turns, 1)
                sp.wait_ge(*shift_in[half].after(d, 0))
                sp.dma_start(q_stack[p][ROW_MAX:ROWS, half * HALF:(half + 1) * HALF, :],
                             shift_dram[half][p].rearrange("s (h q) i -> s h (q i)", q=KB))\
                    .then_inc(shift_in[half].sem, 16)

            def store_parts(n, d, p):
                for half in range(2):
                    sp.wait_ge(*part3[n].after(d, half + 1))
                    sp.dma_start(parts_dram[n][p][:, half * P:half * P + P, :].rearrange("s p t -> p s t"),
                                 split[:, half, :, :]).then_inc(parts_out[n].sem, 16)

            def compact(d, g):
                sp.wait_ge(*normed_done.after(d, g + 1))
                sp.sem_inc(turns, 1)
                sp.wait_ge(*x_shifted.after(d, 0))
                for i in range(GROUP):
                    head = GROUP * g + i
                    row = D * (head % HALF)
                    for m, dst in enumerate((mean, ex2)):
                        sp.dma_start(dst[row:row + D, head // HALF, :],
                                     normed[g % 2][32 * i + D * m:32 * i + D * m + D, :])\
                            .then_inc(moments_in[g % 2].sem, 16)

            def body(b, p):
                o = 1 - p
                for t in range(STEPS):
                    if t == 0 and exists(b + 1):
                        load_stack(b + 1, o, 1)
                    if t == 2:
                        if exists(b - 1):
                            compact(b - 1, 3)
                        if exists(b):
                            load_shift(b, p, 1)
                    if t == 3 and exists(b + 2):
                        store_parts(0, b + 2, p)
                    if t == 7 and exists(b + 2):
                        store_parts(1, b + 2, p)
                    if t == 16 and exists(b):
                        compact(b, 0)
                    if t == 17 and exists(b + 2):
                        load_stack(b + 2, p, 0)
                    if t == 18 and exists(b):
                        compact(b, 1)
                    if t == 20 and exists(b + 1):
                        load_shift(b + 1, o, 0)
                    if t == 26 and exists(b):
                        compact(b, 2)

            iterations(sp, body)

        @block.tensor
        def _(pe):
            pe.wait_ge(weights_in, 16 * 13)
            pe.wait_ge(consts, 4)
            pe.wait_ge(ones_made, 3)

            def claim(b, kind, off, n):
                before = ring_before(b, kind, off, n)
                if before is not None:
                    k, d, m = before
                    tally, per = FREED[k]
                    pe.wait_ge(*tally.after(d, per * (m + 1)))
                return slot(kind, off, n)

            def project(dst, w, cols, data, start_stop=True):
                for c in range(CH):
                    last = nc.tensor.matmul(dst, w[:, c, cols], data[:, c, :], start=(c == 0), stop=(c == CH - 1))
                return last

            def project_T(dst, data, w):
                for kb in range(KB):
                    for c in range(CH):
                        last = nc.tensor.matmul(dst[:, kb // 2, (kb % 2) * C:(kb % 2) * C + C],
                                                data[:, c, kb * P:kb * P + P], w[:, c, :],
                                                start=(c == 0), stop=(c == CH - 1))
                return last

            def filler(b, kind, off, n):
                d = b + off
                ps = claim(b, kind, off, n)
                if kind == "q":
                    pe.wait_ge(*xq_in.after(d, 16))
                    for half in range(CH):
                        last = project(ps[:, half, :], wq_sb, slice(half * P, half * P + P), xs)
                elif kind == "k":
                    pe.wait_ge(*ctxk_in.after(d, 16))
                    for half in range(CH):
                        last = project(ps[:, half, :], wk_sb, slice(half * P, half * P + P), ctx_k)
                elif kind == "v":
                    pe.wait_ge(*ctxv_in.after(d, 16))
                    last = project_T(ps, ctx_v, wv_sb)
                elif kind == "shift":
                    pe.wait_ge(*max_done.after(d, 16 * n + 16))
                    last = nc.tensor.transpose(ps[0:32, 0, 0:P], row_max[:, n, :], ident[:, :])
                elif kind == "k2":
                    pe.wait_ge(*ctx1_in.after(d, 16))
                    last = project(ps[:, 0, :], w1k_sb, slice(0, P), ctx_v)
                elif kind == "v2":
                    last = project_T(ps, ctx_v, w1v_sb)
                elif kind == "q2":
                    pe.wait_ge(*x1_made.after(d, 1))
                    last = project(ps[:, 0, :], w1q_sb, slice(0, P), x1)
                elif kind == "s2":
                    pe.wait_ge(*q2_made.after(d, 1))
                    pe.wait_ge(*k2_made.after(d, 1))
                    for j in range(2):
                        nb = 2 * n + j
                        last = nc.tensor.matmul(ps[:, j, :], q2[:, nb * P:nb * P + P], k2[:, :], start=True, stop=True)
                elif kind == "t2":
                    pe.wait_ge(*probs2_made.after(d, 1))
                    for j in range(2):
                        for nb in range(KB):
                            mb = 2 * n + j
                            last = nc.tensor.transpose(ps[:, j, nb * P:nb * P + P],
                                                       probs2[:, nb, mb * P:mb * P + P], ident[:, :])
                elif kind == "o2":
                    pe.wait_ge(*probs2T_made.after(d, 2))
                    pe.wait_ge(*v2_made.after(d, 1))
                    for mb in range(KB):
                        last = nc.tensor.matmul(ps[:, 0, :], values2[:, mb, n * P:n * P + P], probs2T[:, mb, :],
                                                start=(mb == 0), stop=(mb == KB - 1))
                last.then_inc(made[kind].sem, 1)

            def scores(b, p, t):
                sub, i = divmod(t, GROUP)
                head, kp = GROUP * (sub // 2) + i, sub % 2
                ps = claim(b, "st", 0, t)
                if t == 0:
                    pe.wait_ge(*shift_in[0].after(b, 16))
                if t == 16:
                    pe.wait_ge(*shift_in[1].after(b, 16))
                for j in range(2):
                    kb = 2 * kp + j
                    last = nc.tensor.matmul(ps[:, j, :], k_stack[p][0:ROWS, head, kb * P:kb * P + P],
                                            q_stack[p][0:ROWS, head, :], start=True, stop=True)
                last.then_inc(made["st"].sem, 1)

            def maxima(b, o, t):
                head, qp = divmod(t, 2)
                ps = claim(b, "mx", 1, t)
                if t == 0:
                    pe.wait_ge(*stack_in[0].after(b + 2, 0))
                    pe.wait_ge(*maskrow_in[0].after(b + 2, 0))
                if t == 16:
                    pe.wait_ge(*stack_in[1].after(b + 2, 0))
                    pe.wait_ge(*maskrow_in[1].after(b + 2, 0))
                for j in range(2):
                    qb = 2 * qp + j
                    last = nc.tensor.matmul(ps[:, j, :], q_stack[o][0:ROW_MAX, head, qb * P:qb * P + P],
                                            k_stack[o][0:ROW_MAX, head, :], start=True, stop=True)
                last.then_inc(made["mx"].sem, 1)

            def attend(d, p, sub, quad):
                g, kp = divmod(sub, 2)
                if quad == 0:
                    pe.wait_ge(*exp_done.after(d, GROUP * sub + GROUP))
                    if kp == 0:
                        pe.wait_ge(*normed_done.after(d, g))
                    if sub == 0:
                        pe.wait_ge(*v_squared.after(d, 1))
                if quad == 2:
                    pe.wait_ge(*pair_done.after(d, GROUP * sub + GROUP))
                for i in range(GROUP):
                    rows_ = slice(32 * i, 32 * i + 32)
                    if quad < 2:
                        kb = 2 * kp + quad
                        last = nc.tensor.matmul(att[rows_, :], values[p][:, kb, GROUP * g + i, :],
                                                probs[sub % 2][:, i, quad, :], start=(kb == 0), stop=(kb == KB - 1))
                    else:
                        last = nc.tensor.matmul(den[rows_, :], ones[:, :], pairs[sub % 2][:, i, :],
                                                start=(kp == 0), stop=(kp == 1))
                if quad == 1:
                    last.then_inc(att_done.sem, 1)
                if quad == 2:
                    last.then_inc(den_done.sem, 1)

            def body(b, p):
                for t in range(STEPS):
                    sub, quad = t // GROUP - 1, t % GROUP
                    if exists(b):
                        scores(b, p, t)
                    if quad < 3:
                        if sub < 0 and exists(b - 1):
                            attend(b - 1, 1 - p, SUBS - 1, quad)
                        if sub >= 0 and exists(b):
                            attend(b, p, sub, quad)
                    if exists(b + 1):
                        maxima(b, 1 - p, t)
                    for kind, off, n in FILLERS.get(t, []):
                        if exists(b + off):
                            filler(b, kind, off, n)

            iterations(pe, body)

        @block.scalar
        def _(act):
            act.wait_ge(maskrow_out, 16)

            def exp(b, t):
                sub, i = divmod(t, GROUP)
                if i == 0:
                    act.wait_ge(*att_done.after(b, sub - 1))
                    act.wait_ge(*pair_done.after(b, GROUP * (sub - 1)))
                act.wait_ge(*made["st"].after(b, t + 1))
                nc.scalar.activation(probs[sub % 2][:, i, :, :], slot("st", 0, t), ACT.Exp, scale=SCALE)\
                    .then_inc(exp_done.sem, 1)

            def rows(dram, d):
                return dram[index(d)].rearrange("(c p) t -> p c t", p=P)

            def load_maskrow(d, p, half):
                act.wait_ge(*made["st"].after(d - 2, 16 * half + 16))
                act.wait_ge(*maskrow_in[half].after(d, 0))
                act.dma_start(k_stack[p][ROW_MASK:ROW_MASK + 1, half * HALF:(half + 1) * HALF, :],
                              maskrow_dram[bass.ds(index(d), 1), half * HALF * T:(half + 1) * HALF * T]
                              .rearrange("o (h t) -> o h t", t=T)).then_inc(maskrow_in[half].sem, 16)

            def loads(b, p, t):
                if t == 0 and exists(b + 1):
                    load_maskrow(b + 1, 1 - p, 1)
                if t == 3 and exists(b - 1):
                    if exists(b + 2):
                        act.wait_ge(*made["q"].after(b + 2, 1))
                    act.dma_start(xs[:, :, :], rows(x_in, b - 1)).then_inc(xr_in.sem, 16)
                    act.dma_start(mask_b8[:, :], mask_in[index(b - 1), :].partition_broadcast(P)).then_inc(mask_in_.sem, 16)
                if t == 9 and exists(b + 3):
                    act.wait_ge(*made["k"].after(b + 2, 1))
                    act.dma_start(ctx_k[:, :, :], rows(ctx_in, b + 3)).then_inc(ctxk_in.sem, 16)
                if t == 11 and exists(b - 1):
                    if exists(b + 1):
                        act.wait_ge(*made["v"].after(b + 1, 1))
                    act.dma_start(ctx_v[:, :, :], rows(ctx_in, b - 1)).then_inc(ctx1_in.sem, 16)
                if t == 15 and exists(b + 3):
                    act.wait_ge(*x_centred.after(b - 1, 2))
                    act.dma_start(xs[:, :, :], rows(x_in, b + 3)).then_inc(xq_in.sem, 16)
                if t == 17 and exists(b + 2):
                    load_maskrow(b + 2, p, 0)
                if t == 20 and exists(b + 2):
                    if exists(b + 1):
                        act.wait_ge(*made["v"].after(b + 1, 1))
                    act.wait_ge(*made["v2"].after(b - 1, 1))
                    act.dma_start(ctx_v[:, :, :], rows(ctx_in, b + 2)).then_inc(ctxv_in.sem, 16)
                if t == 31 and exists(b - 1):
                    act.wait_ge(*result_made.after(b - 1, 2))
                    act.dma_start(rows(out, b - 1), x1[:, :, :]).then_inc(result_out.sem, 16)

            def part_2(n, d, half):
                act.wait_ge(*rest_made[n].after(d, half + 1))
                nc.scalar.activation(split[:, half, 1, :], rest[:, :], ACT.Copy).then_inc(part2[n].sem, 1)

            act.wait_ge(consts, 4)
            act.wait_ge(ones_made, 3)
            act.dma_start(xs[:, :, :], rows(x_in, 0)).then_inc(xq_in.sem, 16)
            act.dma_start(ctx_k[:, :, :], rows(ctx_in, 0)).then_inc(ctxk_in.sem, 16)

            def body(b, p):
                d = b - 1
                for t in range(STEPS):
                    if exists(b):
                        exp(b, t)
                    loads(b, p, t)
                    if t in (2, 3) and exists(b + 2):
                        part_2(0, b + 2, t - 2)
                    if t in (6, 7) and exists(b + 2):
                        part_2(1, b + 2, t - 6)
                    if not exists(d):
                        continue
                    if t == 4:
                        act.wait_ge(*mask_in_.after(d, 16))
                        nc.scalar.activation(mask_b[:, :], mask_b8[:, :], ACT.Copy).then_inc(mask_ready.sem, 1)
                    if t == 7:
                        act.wait_ge(*x_masked.after(d, 1))
                        act.wait_ge(*normed_done.after(d, 4))
                        for half in range(CH):
                            act.wait_ge(*x_sumsq.after(d, half))
                            nc.scalar.activation(junk[:, :], xs[:, half, :], ACT.Square,
                                                 accum_out=stats[:, 4 + half:5 + half]).then_inc(x_sumsq.sem, 1)
                    if t == 9:
                        act.wait_ge(*stat_steps.after(d, 5))
                        nc.scalar.activation(spread[:, :], stats[:, 10:12], ACT.Sqrt).then_inc(spread_done.sem, 1)
                        act.wait_ge(*var_clamped.after(d, 1))
                        nc.scalar.activation(ex2[:, :, :], ex2[:, :, :], ACT.Sqrt).then_inc(std_done.sem, 1)
                    if t == 22:
                        for nb in range(KB):
                            if nb % 2 == 0:
                                act.wait_ge(*max2_done.after(d, nb // 2 + 1))
                            if nb == 0:
                                act.wait_ge(*made["t2"].after(d - 1, 2))
                            nc.scalar.activation(probs2[:, nb, :], slot("s2", -1, nb // 2)[:, nb % 2, :], ACT.Exp,
                                                 bias=stats2[:, 0, nb:nb + 1], accum_out=stats2[:, 1, nb:nb + 1])\
                                .then_inc(exp2_done.sem, 1)
                    if t == 26:
                        for n in range(2):
                            act.wait_ge(*made["t2"].after(d, n + 1))
                            if n == 0:
                                act.wait_ge(*made["o2"].after(d - 1, 2))
                            nc.scalar.activation(probs2T[:, 2 * n:2 * n + 2, :], slot("t2", -1, n), ACT.Copy)\
                                .then_inc(probs2T_made.sem, 1)

            iterations(act, body)
            act.wait_ge(*result_out.after(B, 0))

        @block.gpsimd
        def _(pool):
            nc.gpsimd.memset(ident[:, :], 0.0).then_inc(consts, 1)
            pool.wait_ge(consts, 1)
            nc.gpsimd.affine_select(out=ident[:, :], in_=ident[:, :], compare_op=ALU.not_equal, fill=1.0, base=0,
                                    pattern=[[-1, P]], channel_multiplier=1).then_inc(consts, 1)
            for n, stack in enumerate(q_stack):
                pool.wait_ge(consts, 2 + n)
                nc.gpsimd.memset(stack[ROW_MASK:P, :, :].bitcast(fp32), TWO_BF16_ONES).then_inc(consts, 1)

            def part_3(n, d, half):
                pool.wait_ge(*part2[n].after(d, half + 1))
                nc.gpsimd.tensor_tensor(out=split[:, half, 2, :], in0=rest[:, :], in1=split[:, half, 1, :],
                                        op=ALU.subtract).then_inc(part3[n].sem, 1)

            def pair(b, t):
                sub, i = divmod(t, GROUP)
                if i == 0:
                    pool.wait_ge(*den_done.after(b, sub - 1))
                pool.wait_ge(*exp_done.after(b, t + 1))
                nc.gpsimd.tensor_tensor(out=pairs[sub % 2][:, i, :], in0=probs[sub % 2][:, i, 0, :],
                                        in1=probs[sub % 2][:, i, 1, :], op=ALU.add).then_inc(pair_done.sem, 1)

            def body(b, p):
                d = b - 1
                for t in range(STEPS):
                    if exists(b):
                        pair(b, t)
                    if t in (2, 3) and exists(b + 2):
                        part_3(0, b + 2, t - 2)
                    if t in (6, 7) and exists(b + 2):
                        part_3(1, b + 2, t - 6)
                    if t == 10 and exists(b + 1):
                        pool.wait_ge(*v_biased.after(b + 1, 1))
                        v = values[1 - p][:, :, :, :].rearrange("p k h e -> p (k h) e")
                        nc.gpsimd.tensor_tensor(out=v[:, :, D:2 * D], in0=v[:, :, 0:D], in1=v[:, :, 0:D],
                                                op=ALU.mult).then_inc(v_squared.sem, 1)
                    if not exists(d):
                        continue
                    if t == 4:
                        pool.wait_ge(*mask_ready.after(d, 1))
                        pool.wait_ge(*xr_in.after(d, 16))
                        nc.gpsimd.tensor_tensor(out=xs[:, :, :], in0=xs[:, :, :],
                                                in1=mask_b[:, :].unsqueeze(1).to_broadcast([P, CH, T]),
                                                op=ALU.mult).then_inc(x_masked.sem, 1)
                    if t == 5:
                        pool.wait_ge(*moments_in[0].after(d + 1, 0))
                        pool.wait_ge(*moments_in[1].after(d + 1, 0))
                        pool.wait_ge(*made["o2"].after(d - 1, 2))
                        nc.gpsimd.tensor_tensor(out=square[:, 0:CH, :], in0=mean[:, :, :], in1=mean[:, :, :],
                                                op=ALU.mult).then_inc(mean_squared.sem, 1)
                        pool.wait_ge(*mean_squared.after(d, 1))
                        nc.gpsimd.tensor_tensor(out=ex2[:, :, :], in0=ex2[:, :, :], in1=square[:, 0:CH, :],
                                                op=ALU.subtract).then_inc(var_made.sem, 1)
                    if t == 13:
                        pool.wait_ge(*x_styled.after(d, 2))
                        nc.gpsimd.tensor_tensor(out=x1[:, :, :], in0=x1[:, :, :], in1=mean[:, :, :],
                                                op=ALU.add).then_inc(x_shifted.sem, 1)
                        pool.wait_ge(*x_shifted.after(d, 1))
                        nc.gpsimd.tensor_tensor(out=x1[:, :, :], in0=x1[:, :, :],
                                                in1=mask_b[:, :].unsqueeze(1).to_broadcast([P, CH, T]),
                                                op=ALU.mult).then_inc(x1_made.sem, 1)

            iterations(pool, body)

        @block.vector
        def _(dve):
            nc.vector.memset(ones[:, :], 1.0).then_inc(ones_made, 1)
            for stack in k_stack:
                nc.vector.memset(stack[ROW_MASK:P, :, :].bitcast(fp32), TWO_BF16_ONES).then_inc(ones_made, 1)
            dve.wait_ge(weights_in, 16 * 13)
            nc.vector.tensor_scalar(mask_f, mask_u8[:, :], 1.0, MASKED, ALU.subtract, ALU.mult)\
                .then_inc(mask_scaled, 1)
            dve.wait_ge(mask_scaled, 1)
            for h in range(HEADS):
                nc.vector.tensor_copy(maskrow[:, h * T:h * T + T], mask_f).then_inc(maskrow_made, 1)
            dve.wait_ge(maskrow_out, 16)

            def split_first(n, kind, d, half, bias):
                ps = slot(kind, 2, 0)[:, half, :]
                if half == 0:
                    dve.wait_ge(*made[kind].after(d, 1))
                    if n == 0:
                        dve.wait_ge(*parts_out[1].after(d, 0))
                        dve.wait_ge(*part3[1].after(d, 0))
                    else:
                        dve.wait_ge(*parts_out[0].after(d, 32))
                        dve.wait_ge(*part3[0].after(d, 2))
                nc.vector.tensor_scalar(split[:, half, 0, :], ps, bias[:, half:half + 1], None, ALU.add)\
                    .then_inc(part1[n].sem, 1)
                dve.wait_ge(*part1[n].after(d, half + 1))
                if half == 1:
                    dve.wait_ge(*part3[n].after(d, 1))
                nc.vector.scalar_tensor_tensor(out=rest[:, :], in0=ps, scalar=bias[:, half:half + 1],
                                               in1=split[:, half, 0, :], op0=ALU.add, op1=ALU.subtract)\
                    .then_inc(rest_made[n].sem, 1)

            def add_value_bias(d, kind, off, done, dst, bias):
                dve.wait_ge(*made[kind].after(d, 1))
                ps = slot(kind, off, 0)
                for half in range(2):
                    src = ps[:, half, :].rearrange("p (k c) -> p k c", k=2)
                    bc = bias[:, :].unsqueeze(1).to_broadcast([P, 2, C])
                    if kind == "v":
                        for j in range(2):
                            last = nc.vector.tensor_tensor(
                                out=dst[:, 2 * half + j, :, 0:D],
                                in0=src[:, j, :].rearrange("p (h d) -> p h d", d=D),
                                in1=bias[:, :].rearrange("p (h d) -> p h d", d=D), op=ALU.add)
                    else:
                        last = nc.vector.tensor_tensor(out=dst[:, 2 * half:2 * half + 2, :], in0=src, in1=bc, op=ALU.add)
                last.then_inc(done.sem, 1)

            def shift_rows(d, off, half):
                ps = slot("shift", off, half)[0:32, 0, 0:P]
                dve.wait_ge(*made["shift"].after(d, half + 1))
                dve.wait_ge(*shift_out[1 - half].after(d + half - 1, 16))
                nc.vector.tensor_scalar(neg_max[:, 0, :], ps, -1.0, None, ALU.mult).then_inc(neg1.sem, 1)
                dve.wait_ge(*neg1.after(d, half + 1))
                nc.vector.scalar_tensor_tensor(out=neg_rest[:, :], in0=ps, scalar=-1.0, in1=neg_max[:, 0, :],
                                               op0=ALU.mult, op1=ALU.subtract).then_inc(shift_rest.sem, 1)
                dve.wait_ge(*shift_rest.after(d, half + 1))
                nc.vector.tensor_copy(neg_max[:, 1, :], neg_rest[:, :]).then_inc(neg2.sem, 1)
                dve.wait_ge(*neg2.after(d, half + 1))
                nc.vector.tensor_tensor(out=neg_max[:, 2, :], in0=neg_rest[:, :], in1=neg_max[:, 1, :],
                                        op=ALU.subtract).then_inc(neg3.sem, 1)

            def normalise(d, g):
                dve.wait_ge(*den_done.after(d, 2 * g + 2))
                dve.wait_ge(*normed_done.after(d, g))
                if g == 0:
                    dve.wait_ge(*x_sumsq.after(d - 1, 2))
                nc.vector.reciprocal(recip[:, :], den[:, :]).then_inc(recip_done.sem, 1)
                dve.wait_ge(*recip_done.after(d, g + 1))
                dve.wait_ge(*moments_in[g % 2].after(d, 16 * 2 * GROUP * (g // 2)))
                nc.vector.tensor_tensor(out=normed[g % 2][:, :], in0=att[:, :], in1=recip[:, :], op=ALU.mult)\
                    .then_inc(normed_done.sem, 1)

            def instance_stats(d):
                s = stats
                dve.wait_ge(*n_valid.after(d, 1))
                nc.vector.reciprocal(s[:, 1:2], s[:, 0:1]).then_inc(stat_steps.sem, 1)
                dve.wait_ge(*stat_steps.after(d, 1))
                dve.wait_ge(*x_sum.after(d, 1))
                nc.vector.tensor_scalar(s[:, 6:8], s[:, 2:4], s[:, 1:2], None, ALU.mult).then_inc(stat_steps.sem, 1)
                dve.wait_ge(*x_sumsq.after(d, 2))
                dve.wait_ge(*stat_steps.after(d, 2))
                nc.vector.tensor_tensor(out=s[:, 8:10], in0=s[:, 6:8], in1=s[:, 6:8], op=ALU.mult)\
                    .then_inc(stat_steps.sem, 1)
                dve.wait_ge(*stat_steps.after(d, 3))
                nc.vector.scalar_tensor_tensor(out=s[:, 10:12], in0=s[:, 4:6], scalar=s[:, 1:2], in1=s[:, 8:10],
                                               op0=ALU.mult, op1=ALU.subtract).then_inc(stat_steps.sem, 1)
                dve.wait_ge(*stat_steps.after(d, 4))
                nc.vector.tensor_scalar(s[:, 10:12], s[:, 10:12], 0.0, EPS, ALU.max, ALU.add)\
                    .then_inc(stat_steps.sem, 1)

            def split_q2(d):
                ps = slot("q2", -1, 0)[:, 0, :]
                dve.wait_ge(*made["q2"].after(d, 1))
                dve.wait_ge(*made["s2"].after(d - 1, 2))
                nc.vector.tensor_scalar(q2[:, :], ps, b1q_sb[:, :], None, ALU.add).then_inc(q2_hi.sem, 1)
                dve.wait_ge(*q2_hi.after(d, 1))
                nc.vector.scalar_tensor_tensor(out=q2[64:128, :], in0=ps[64:128], scalar=b1q_sb[64:128, :],
                                               in1=q2[64:128, :].bitcast(fp32), op0=ALU.add, op1=ALU.subtract)\
                    .then_inc(q2_made.sem, 1)

            def split_k2(d):
                ps = slot("k2", -1, 0)[:, 0, :]
                dve.wait_ge(*made["k2"].after(d, 1))
                dve.wait_ge(*made["s2"].after(d - 1, 2))
                nc.vector.tensor_scalar(k2[:, :], ps, b1k_sb[:, :], None, ALU.add).then_inc(k2_hi.sem, 1)
                dve.wait_ge(*k2_hi.after(d, 1))
                for lo in (32, 96):
                    last = nc.vector.scalar_tensor_tensor(
                        out=k2[lo:lo + 32, :], in0=ps[lo:lo + 32], scalar=b1k_sb[lo:lo + 32, :],
                        in1=k2[lo:lo + 32, :].bitcast(fp32), op0=ALU.add, op1=ALU.subtract)
                    last.then_inc((k2_hi if lo == 32 else k2_made).sem, 1)

            def body(b, p):
                d = b - 1
                for t in range(STEPS):
                    if t % 8 == 3:
                        g = t // 8 - 1
                        if g < 0 and exists(d):
                            normalise(d, 3)
                        if g >= 0 and exists(b):
                            normalise(b, g)
                    if exists(b + 1):
                        dve.wait_ge(*made["mx"].after(b + 1, t + 1))
                        if t % 16 == 0:
                            dve.wait_ge(*made["shift"].after(b, t // 16 + 1))
                        nc.vector.reduce_max(row_max[:, t // 16, 2 * (t % 16):2 * (t % 16) + 2], slot("mx", 1, t),
                                             axis=AX.X).then_inc(max_done.sem, 1)
                    if t == 1:
                        if exists(b):
                            shift_rows(b, 0, 1)
                        if exists(b + 2):
                            split_first(0, "q", b + 2, 0, bq_sb)
                            split_first(0, "q", b + 2, 1, bq_sb)
                    if t == 5 and exists(b + 2):
                        split_first(1, "k", b + 2, 0, bk_sb)
                        split_first(1, "k", b + 2, 1, bk_sb)
                    if t == 9 and exists(b + 1):
                        dve.wait_ge(*att_done.after(b - 1, SUBS))
                        add_value_bias(b + 1, "v", 1, v_biased, values[1 - p], bv_sb)
                    if t == 17 and exists(b + 1):
                        shift_rows(b + 1, 1, 0)
                    if not exists(d):
                        continue
                    if t == 7:
                        dve.wait_ge(*mask_ready.after(d, 1))
                        nc.vector.reduce_sum(stats[:, 0:1], mask_b[:, :], axis=AX.X).then_inc(n_valid.sem, 1)
                        dve.wait_ge(*x_masked.after(d, 1))
                        nc.vector.reduce_sum(stats[:, 2:4], xs[:, :, :], axis=AX.X).then_inc(x_sum.sem, 1)
                    if t == 8:
                        instance_stats(d)
                        dve.wait_ge(*var_made.after(d, 1))
                        nc.vector.tensor_scalar(ex2[:, :, :], ex2[:, :, :], 0.0, None, ALU.max)\
                            .then_inc(var_clamped.sem, 1)
                    if t == 11:
                        dve.wait_ge(*spread_done.after(d, 1))
                        nc.vector.reciprocal(stats[:, 12:14], spread[:, :]).then_inc(stat_steps.sem, 1)
                        dve.wait_ge(*result_out.after(d, 0))
                        for half in range(CH):
                            nc.vector.scalar_tensor_tensor(out=x1[:, half, :], in0=xs[:, half, :],
                                                           scalar=stats[:, 6 + half:7 + half], in1=mask_b[:, :],
                                                           op0=ALU.subtract, op1=ALU.mult).then_inc(x_centred.sem, 1)
                        dve.wait_ge(*stat_steps.after(d, 6))
                        dve.wait_ge(*std_done.after(d, 1))
                        for half in range(CH):
                            dve.wait_ge(*x_centred.after(d, half + 1))
                            nc.vector.scalar_tensor_tensor(out=x1[:, half, :], in0=x1[:, half, :],
                                                           scalar=stats[:, 12 + half:13 + half], in1=ex2[:, half, :],
                                                           op0=ALU.mult, op1=ALU.mult).then_inc(x_styled.sem, 1)
                        nc.vector.memset(stats[:, 14:15], 0.0).then_inc(stat_steps.sem, 1)
                    if t == 13:
                        split_k2(d)
                    if t == 17:
                        dve.wait_ge(*made["o2"].after(d - 1, 2))
                        add_value_bias(d, "v2", -1, v2_made, values2, b1v_sb)
                    if t == 18:
                        split_q2(d)
                    if t == 21:
                        for n in range(2):
                            dve.wait_ge(*made["s2"].after(d, n + 1))
                            nc.vector.reduce_max(stats2[:, 0, 2 * n:2 * n + 2], slot("s2", -1, n), axis=AX.X,
                                                 negate=True).then_inc(max2_done.sem, 1)
                    if t == 24:
                        dve.wait_ge(*exp2_done.after(d, KB))
                        nc.vector.reciprocal(stats2[:, 2, :], stats2[:, 1, :]).then_inc(sum2_inv.sem, 1)
                        dve.wait_ge(*sum2_inv.after(d, 1))
                        for nb in range(KB):
                            last = nc.vector.tensor_scalar(probs2[:, nb, :], probs2[:, nb, :], stats2[:, 2, nb:nb + 1],
                                                           None, ALU.mult)
                        last.then_inc(probs2_made.sem, 1)
                    if t == 29:
                        for n in range(CH):
                            dve.wait_ge(*made["o2"].after(d, n + 1))
                            nc.vector.tensor_tensor(out=x1[:, n, :], in0=slot("o2", -1, n)[:, 0, :], in1=x1[:, n, :],
                                                    op=ALU.add).then_inc(result_made.sem, 1)

            iterations(dve, body)


def kernel(x, ctx_2048, mask_Bx1x2048_bf1, L0_xattn_Wq, L0_xattn_bq, L0_xattn_Wk, L0_xattn_bk, L0_xattn_Wv,
           L0_xattn_bv, L1_xattn_Wq, L1_xattn_bq, L1_xattn_Wk, L1_xattn_bk, L1_xattn_Wv, L1_xattn_bv):
    import numpy as np
    import concourse.bacc as bacc
    from concourse import mybir
    from concourse.bass_utils import run_bass_kernel_spmd

    def T_(w):
        return np.ascontiguousarray(np.asarray(w).T)

    def halves(v):
        return np.ascontiguousarray(np.asarray(v).reshape(2, 128).T)

    arrays = dict(
        x=np.ascontiguousarray(x), ctx=np.ascontiguousarray(ctx_2048),
        mask=np.ascontiguousarray(mask_Bx1x2048_bf1).reshape(16, 512).view(np.uint8),
        wqT=T_(L0_xattn_Wq), bq=halves(L0_xattn_bq), wkT=T_(L0_xattn_Wk), bk=halves(L0_xattn_bk),
        wvT=T_(L0_xattn_Wv), bv=np.ascontiguousarray(L0_xattn_bv),
        w1qT=np.tile(T_(L1_xattn_Wq), (1, 4)), b1q=np.tile(np.asarray(L1_xattn_bq), 4).reshape(128, 1),
        w1kT=np.tile(T_(L1_xattn_Wk), (1, 4)), b1k=np.tile(np.asarray(L1_xattn_bk), 4).reshape(128, 1),
        w1vT=T_(L1_xattn_Wv), b1v=np.ascontiguousarray(L1_xattn_bv))
    nc = bacc.Bacc("TRN2", target_bir_lowering=False, num_devices=1)
    args = [nc.dram_tensor(f"{n}_dram", a.shape, mybir.dt.from_np(a.dtype), kind="ExternalInput").ap()
            for n, a in arrays.items()]
    out = nc.dram_tensor("out_dram", (16, 256, 512), mybir.dt.float32, kind="ExternalOutput").ap()
    build(nc, *args, out)
    r = run_bass_kernel_spmd(nc, [{f"{n}_dram": a for n, a in arrays.items()}], core_ids=[0])
    return r.results[0]["out_dram"]
```

```python
import concourse.bass as bass
from concourse import mybir
from contextlib import ExitStack

B, C, T = 16, 256, 512
HEADS, D = 16, 16
D1 = 32
P = 128
CH = C // P
KB = T // P
HALF = HEADS // 2
STEPS = 2 * HEADS
GROUP = 4
SUBS = STEPS // GROUP
PARTS = 3
Q_PARTS = (0, 1, 0, 1, 0, 2)
K_PARTS = (0, 0, 1, 1, 2, 0)
ROW_MASK = D * len(Q_PARTS)
ROW_MAX = ROW_MASK + 1
ROWS = ROW_MAX + PARTS
SCALE = 1.0 / float(D) ** 0.5
MASKED = 3.0e38
TWO_BF16_ONES = 1.0 + 0x3F80 * 2.0 ** -23
EPS = 1e-5
RING = 3

FILLERS = {
    0: [("q", 2, 0)],
    1: [("shift", 0, 1), ("o2", -2, 0)],
    2: [("q", 2, 1)],
    3: [("o2", -2, 1)],
    6: [("k", 2, 0)],
    8: [("k", 2, 1)],
    9: [("v", 1, 0)],
    13: [("k2", -1, 0)],
    15: [("v2", -1, 0)],
    16: [("shift", 1, 0)],
    19: [("v2", -1, 1)],
    21: [("q2", -1, 0)],
    23: [("s2", -1, 0)],
    24: [("s2", -1, 1)],
    28: [("t2", -1, 0), ("t2", -1, 1)],
}
JOBS = []
for _t in range(STEPS):
    JOBS += [("st", 0, _t), ("mx", 1, _t)] + FILLERS.get(_t, [])
assert len(JOBS) % RING == 0
assert all(kind in ("st", "mx") for kind, _, _ in JOBS[-RING:])
FIRST, LAST = -2, B + 1
LOOP_FROM, LOOP_TO = 3, B - 3

LOOP_I = 8


class Looped:

    def __init__(self, i, c):
        self.i, self.c = i, c

    def __add__(self, n):
        return Looped(self.i, self.c + n)

    def __sub__(self, n):
        return Looped(self.i, self.c - n)

    def times(self, per, n):
        return self.i * (2 * per) + (self.c * per + n)


def index(d):
    return d if isinstance(d, int) else d.times(1, 0)


def exists(d):
    return not isinstance(d, int) or 0 <= d < B


def ring_place(kind, off, n):
    return JOBS.index((kind, off, n)) % RING


def ring_before(b, kind, off, n):
    at = JOBS.index((kind, off, n))
    back = 0
    while True:
        at -= RING
        if at < 0:
            at += len(JOBS)
            back += 1
        k, o, m = JOBS[at]
        d = b - back + o
        if isinstance(b, int) and b - back < FIRST:
            return None
        if exists(d):
            return k, d, m


def build(nc, x_in, ctx_in, mask_in, wqT, bq, wkT, bk, wvT, bv, w1qT, b1q, w1kT, b1k, w1vT, b1v, out):
    fp32, bf16, fp32r = mybir.dt.float32, mybir.dt.bfloat16, mybir.dt.float32r
    ALU, ACT, AX = mybir.AluOpType, mybir.ActivationFunctionType, mybir.AxisListType

    parts_dram = [[nc.dram_tensor(f"parts_{n}{p}", (PARTS, C, T), bf16, kind="Internal").ap()
                   for p in range(2)] for n in "qk"]
    shift_dram = [[nc.dram_tensor(f"shift_{h}{p}", (PARTS, HALF * KB, P), bf16, kind="Internal").ap()
                   for p in range(2)] for h in range(2)]
    inv_dram = nc.dram_tensor("inv_dram", (HEADS, T), fp32, kind="Internal").ap()
    maskrow_dram = nc.dram_tensor("maskrow", (B, HEADS * T), bf16, kind="Internal").ap()

    ctx = ExitStack()
    with ctx:
        def sb(name, shape, dt):
            return ctx.enter_context(nc.sbuf_tensor(name, shape, dt))

        def sem(name):
            return ctx.enter_context(nc.semaphore(name))

        class Tally:

            def __init__(self, name, per):
                self.sem, self.per = sem(name), per

            def after(self, d, n):
                return self.sem, (max(d * self.per + n, 0) if isinstance(d, int) else d.times(self.per, n))

        turns = sem("turns")

        wq_sb, wk_sb = sb("wq_sb", [P, CH, C], fp32), sb("wk_sb", [P, CH, C], fp32)
        wv_sb, w1v_sb = sb("wv_sb", [P, CH, C], fp32), sb("w1v_sb", [P, CH, C], fp32)
        w1q_sb, w1k_sb = sb("w1q_sb", [P, CH, P], fp32), sb("w1k_sb", [P, CH, P], fp32)
        bq_sb, bk_sb = sb("bq_sb", [P, CH], fp32), sb("bk_sb", [P, CH], fp32)
        b1q_sb, b1k_sb = sb("b1q_sb", [P, 1], fp32), sb("b1k_sb", [P, 1], fp32)
        bv_sb, b1v_sb = sb("bv_sb", [P, C], fp32), sb("b1v_sb", [P, C], fp32)
        ident, pick = sb("ident", [P, P], fp32), sb("pick", [P, SUBS // 2, 32], fp32)
        mask_u8 = sb("mask_u8", [B, T], mybir.dt.uint8)
        xs, ctx_k = sb("xs", [P, CH, T], fp32), sb("ctx_k", [P, CH, T], fp32)
        ctx_v = sb("ctx_v", [P, CH, T], fp32)
        split, rest = sb("split", [P, CH, PARTS, T], bf16), sb("rest", [P, T], fp32)
        q_stack = [sb(f"q_stack{p}", [P, HEADS, T], bf16) for p in range(2)]
        k_stack = [sb(f"k_stack{p}", [P, HEADS, T], bf16) for p in range(2)]
        row_max = sb("row_max", [P, 2, HALF * KB], fp32)
        neg_max, neg_rest = sb("neg_max", [32, PARTS, P], bf16), sb("neg_rest", [32, P], fp32)
        values = [sb(f"values{p}", [P, KB, HEADS, 2 * D], fp32) for p in range(2)]
        probs = [sb(f"probs{p}", [P, GROUP, 2, T], fp32) for p in range(2)]
        pairs = [sb(f"pairs{p}", [P, GROUP, T], fp32) for p in range(2)]
        raw = [sb(f"raw{p}", [P, T], fp32) for p in range(2)]
        inv_rows = sb("inv_rows", [P, T], fp32)
        mean, ex2 = sb("mean", [P, CH, T], fp32), sb("ex2", [P, CH, T], fp32)
        mask_b8, mask_b = sb("mask_b8", [P, T], mybir.dt.uint8), sb("mask_b", [P, T], fp32)
        stats, spread = sb("stats", [P, 16], fp32), sb("spread", [P, CH], fp32)
        x1 = sb("x1", [P, CH, T], fp32)
        q2, k2 = sb("q2", [P, T], fp32r), sb("k2", [P, T], fp32r)
        values2 = sb("values2", [P, KB, C], fp32)
        probs2, probs2T = sb("probs2", [P, KB, T], fp32), sb("probs2T", [P, KB, T], fp32)
        stats2 = sb("stats2", [P, 3, KB], fp32)
        mask_f = probs[1][0:B, 0, 0, :]
        maskrow = probs[0][0:B, :, :, :].rearrange("p a b t -> p (a b t)").bitcast(bf16)[:, 0:HEADS * T]
        square = probs2T
        inv_den = x1

        ring = ctx.enter_context(nc.psum_tensor("ring", [P, RING, 2, T], fp32))
        att = ctx.enter_context(nc.psum_tensor("att", [P, T], fp32))
        den = ctx.enter_context(nc.psum_tensor("den", [P, T], fp32))

        pick_cleared = sem("pick_cleared")
        ONES = SUBS // 2 + len(k_stack)
        weights_in, consts, ones_made, mask_scaled = sem("weights_in"), sem("consts"), sem("ones_made"), sem("mask_scaled")
        maskrow_made, maskrow_out = sem("maskrow_made"), sem("maskrow_out")
        xq_in, xr_in = Tally("xq_in", 16), Tally("xr_in", 16)
        ctxk_in, ctxv_in, ctx1_in = Tally("ctxk_in", 16), Tally("ctxv_in", 16), Tally("ctx1_in", 16)
        mask_in_ = Tally("mask_in_", 16)
        parts_out = [Tally(f"parts_out_{n}", 32) for n in "qk"]
        stack_in = [Tally(f"stack_in{h}", 16 * 2 * len(Q_PARTS)) for h in range(2)]
        maskrow_in = [Tally(f"maskrow_in{h}", 16) for h in range(2)]
        shift_out = [Tally(f"shift_out{h}", 16) for h in range(2)]
        shift_in = [Tally(f"shift_in{h}", 16) for h in range(2)]
        moments_in = [Tally(f"moments_in{n}", 16 * HEADS) for n in range(2)]
        inv_out, inv_in = Tally("inv_out", 16 * GROUP), Tally("inv_in", 16 * CH)
        result_out = Tally("result_out", 16)
        made = {k: Tally(f"made_{k}", n) for k, n in dict(
            st=STEPS, mx=STEPS, q=2, k=2, v=1, shift=2, k2=1, v2=2, q2=1, s2=2, t2=2, o2=2).items()}
        att_done, den_done = Tally("att_done", SUBS), Tally("den_done", SUBS)
        exp_done, max_done = Tally("exp_done", STEPS), Tally("max_done", STEPS)
        rest_made = [Tally(f"rest_made_{n}", 2) for n in "qk"]
        v_biased, shift_rest = Tally("v_biased", 1), Tally("shift_rest", 2)
        k2_made, v2_made, q2_made = Tally("k2_made", 1), Tally("v2_made", 2), Tally("q2_made", 1)
        exp2_done, probs2T_made, result_made = Tally("exp2_done", KB), Tally("probs2T_made", 2), Tally("result_made", 2)
        FREED = dict(st=(exp_done, 1), mx=(max_done, 1), q=(rest_made[0], 1), k=(rest_made[1], 1),
                     v=(v_biased, 1), shift=(shift_rest, 1), k2=(k2_made, 1), v2=(v2_made, 1),
                     q2=(q2_made, 1), s2=(exp2_done, 2), t2=(probs2T_made, 1), o2=(result_made, 1))
        part1 = [Tally(f"part1_{n}", 2) for n in "qk"]
        part2 = [Tally(f"part2_{n}", 2) for n in "qk"]
        part3 = [Tally(f"part3_{n}", 2) for n in "qk"]
        neg1, neg2, neg3 = Tally("neg1", 2), Tally("neg2", 2), Tally("neg3", 2)
        v_squared, pair_done = Tally("v_squared", 2), Tally("pair_done", STEPS)
        att_copied, den_copied, inv_made = Tally("att_copied", 4), Tally("den_copied", 1), Tally("inv_made", 4)
        mask_ready, x_masked = Tally("mask_ready", 1), Tally("x_masked", 2)
        n_valid, x_sum, x_sumsq = Tally("n_valid", 1), Tally("x_sum", 1), Tally("x_sumsq", 2)
        stat_steps = Tally("stat_steps", 6)
        spread_done, std_done = Tally("spread_done", 1), Tally("std_done", 1)
        mean_made, ex2_made = Tally("mean_made", 2), Tally("ex2_made", 2)
        mean_squared, var_made, var_clamped = Tally("mean_squared", 1), Tally("var_made", 2), Tally("var_clamped", 1)
        x_scaled, x_shifted, x1_made = Tally("x_scaled", 2), Tally("x_shifted", 2), Tally("x1_made", 2)
        q2_hi, k2_hi = Tally("q2_hi", 1), Tally("k2_hi", 2)
        max2_done, sum2_inv, probs2_made = Tally("max2_done", 2), Tally("sum2_inv", 1), Tally("probs2_made", 1)

        def slot(kind, off, n):
            return ring[:, ring_place(kind, off, n)]

        def iterations(eng, body):
            for b in range(FIRST, LOOP_FROM):
                body(b, b % 2)
            with eng.Fori(LOOP_I, LOOP_I + (LOOP_TO - LOOP_FROM) // 2) as i:
                body(Looped(i, LOOP_FROM - 2 * LOOP_I), LOOP_FROM % 2)
                body(Looped(i, LOOP_FROM + 1 - 2 * LOOP_I), (LOOP_FROM + 1) % 2)
            for b in range(LOOP_TO, LAST + 1):
                body(b, b % 2)

        block = ctx.enter_context(nc.Block())

        @block.sync
        def _(sp):
            for dst, src in ((wq_sb, wqT), (wk_sb, wkT), (wv_sb, wvT), (w1v_sb, w1vT), (w1q_sb, w1qT), (w1k_sb, w1kT)):
                sp.dma_start(dst[:, :, :], src.rearrange("(c p) o -> p c o", p=P)).then_inc(weights_in, 16)
            for dst, src in ((bq_sb, bq), (bk_sb, bk), (b1q_sb, b1q), (b1k_sb, b1k)):
                sp.dma_start(dst[:, :], src).then_inc(weights_in, 16)
            for dst, src in ((bv_sb, bv), (b1v_sb, b1v)):
                sp.dma_start(dst[:, :], src.partition_broadcast(P)).then_inc(weights_in, 16)
            sp.dma_start(mask_u8[:, :], mask_in).then_inc(weights_in, 16)
            sp.wait_ge(consts, 4)
            sp.wait_ge(ones_made, ONES)
            sp.wait_ge(maskrow_made, HEADS)
            sp.dma_start(maskrow_dram, maskrow).then_inc(maskrow_out, 16)
            sp.wait_ge(maskrow_out, 16)

            def load_stack(d, p, half):
                sp.wait_ge(*made["st"].after(d - 2, 16 * half + 16))
                sp.sem_inc(turns, 1)
                sp.wait_ge(*stack_in[half].after(d, 0))
                sp.sem_inc(turns, 1)
                sp.wait_ge(*parts_out[0].after(d, 32))
                sp.sem_inc(turns, 1)
                sp.wait_ge(*parts_out[1].after(d, 32))
                here = slice(half * HALF, half * HALF + HALF)
                for n, (stack, order) in enumerate(((q_stack[p], Q_PARTS), (k_stack[p], K_PARTS))):
                    for j, part in enumerate(order):
                        src = parts_dram[n][p][part, half * P:half * P + P, :]
                        sp.dma_start(stack[D * j:D * j + D, here, :], src.rearrange("(h d) t -> d h t", d=D))\
                            .then_inc(stack_in[half].sem, 16)

            def load_shift(d, p, half):
                sp.wait_ge(*neg3.after(d, half + 1))
                sp.sem_inc(turns, 1)
                sp.wait_ge(*shift_out[half].after(d, 0))
                sp.dma_start(shift_dram[half][p].rearrange("s r i -> r s i"), neg_max[:, :, :])\
                    .then_inc(shift_out[half].sem, 16)
                sp.wait_ge(*shift_out[half].after(d, 16))
                sp.sem_inc(turns, 1)
                sp.wait_ge(*shift_in[half].after(d, 0))
                sp.dma_start(q_stack[p][ROW_MAX:ROWS, half * HALF:(half + 1) * HALF, :],
                             shift_dram[half][p].rearrange("s (h q) i -> s h (q i)", q=KB))\
                    .then_inc(shift_in[half].sem, 16)

            def store_parts(n, d, p):
                for half in range(2):
                    sp.wait_ge(*part3[n].after(d, half + 1))
                    sp.dma_start(parts_dram[n][p][:, half * P:half * P + P, :].rearrange("s p t -> p s t"),
                                 split[:, half, :, :]).then_inc(parts_out[n].sem, 16)

            def compact(d, g):
                sp.wait_ge(*att_copied.after(d, g + 1))
                sp.sem_inc(turns, 1)
                sp.wait_ge(*x_shifted.after(d, 0))
                for i in range(GROUP):
                    head = GROUP * g + i
                    row = D * (head % HALF)
                    for m, dst in enumerate((mean, ex2)):
                        sp.dma_start(dst[row:row + D, head // HALF, :],
                                     raw[g % 2][32 * i + D * m:32 * i + D * m + D, :])\
                            .then_inc(moments_in[g % 2].sem, 16)

            def spread_inverses(d):
                sp.wait_ge(*inv_made.after(d, 4))
                sp.sem_inc(turns, 1)
                sp.wait_ge(*inv_out.after(d, 0))
                sp.sem_inc(turns, 1)
                sp.wait_ge(*inv_in.after(d, 0))
                for i in range(GROUP):
                    sp.dma_start(inv_dram.rearrange("(g i) t -> i g t", i=GROUP)[i],
                                 inv_rows[32 * i:32 * i + HEADS // GROUP, :]).then_inc(inv_out.sem, 16)
                sp.wait_ge(*inv_out.after(d, 16 * GROUP))
                sp.sem_inc(turns, 1)
                sp.wait_ge(*result_out.after(d, 0))
                for half in range(CH):
                    sp.dma_start(inv_den[:, half, :],
                                 inv_dram[half * HALF:half * HALF + HALF, :].unsqueeze(1).to_broadcast([HALF, D, T]))\
                        .then_inc(inv_in.sem, 16)

            def body(b, p):
                o = 1 - p
                for t in range(STEPS):
                    if t == 0 and exists(b + 1):
                        load_stack(b + 1, o, 1)
                    if t == 2:
                        if exists(b - 1):
                            compact(b - 1, 3)
                        if exists(b):
                            load_shift(b, p, 1)
                    if t == 4 and exists(b + 2):
                        store_parts(0, b + 2, p)
                    if t == 6 and exists(b - 1):
                        spread_inverses(b - 1)
                    if t == 10 and exists(b + 2):
                        store_parts(1, b + 2, p)
                    if t == 17 and exists(b + 2):
                        load_stack(b + 2, p, 0)
                    if t == 18 and exists(b):
                        compact(b, 0)
                        compact(b, 1)
                    if t == 20 and exists(b + 1):
                        load_shift(b + 1, o, 0)
                    if t == 26 and exists(b):
                        compact(b, 2)

            iterations(sp, body)

        @block.tensor
        def _(pe):
            pe.wait_ge(weights_in, 16 * 13)
            pe.wait_ge(consts, 4)
            pe.wait_ge(ones_made, ONES)

            def claim(b, kind, off, n):
                before = ring_before(b, kind, off, n)
                if before is not None:
                    k, d, m = before
                    tally, per = FREED[k]
                    pe.wait_ge(*tally.after(d, per * (m + 1)))
                return slot(kind, off, n)

            def project(dst, w, cols, data, start_stop=True):
                for c in range(CH):
                    last = nc.tensor.matmul(dst, w[:, c, cols], data[:, c, :], start=(c == 0), stop=(c == CH - 1))
                return last

            def project_T(dst, data, w, blocks):
                for j, kb in enumerate(blocks):
                    for c in range(CH):
                        last = nc.tensor.matmul(dst[:, j // 2, (j % 2) * C:(j % 2) * C + C],
                                                data[:, c, kb * P:kb * P + P], w[:, c, :],
                                                start=(c == 0), stop=(c == CH - 1))
                return last

            def filler(b, kind, off, n):
                d = b + off
                ps = claim(b, kind, off, n)
                if kind == "q":
                    pe.wait_ge(*xq_in.after(d, 16))
                    last = project(ps[:, 0, :], wq_sb, slice(n * P, n * P + P), xs)
                elif kind == "k":
                    pe.wait_ge(*ctxk_in.after(d, 16))
                    last = project(ps[:, 0, :], wk_sb, slice(n * P, n * P + P), ctx_k)
                elif kind == "v":
                    pe.wait_ge(*ctxv_in.after(d, 16))
                    last = project_T(ps, ctx_v, wv_sb, range(KB))
                elif kind == "shift":
                    pe.wait_ge(*max_done.after(d, 16 * n + 16))
                    last = nc.tensor.transpose(ps[0:32, 0, 0:P], row_max[:, n, :], ident[:, :])
                elif kind == "k2":
                    pe.wait_ge(*ctx1_in.after(d, 16))
                    last = project(ps[:, 0, :], w1k_sb, slice(0, P), ctx_v)
                elif kind == "v2":
                    last = project_T(ps, ctx_v, w1v_sb, range(2 * n, 2 * n + 2))
                elif kind == "q2":
                    pe.wait_ge(*x1_made.after(d, 2))
                    last = project(ps[:, 0, :], w1q_sb, slice(0, P), x1)
                elif kind == "s2":
                    pe.wait_ge(*q2_made.after(d, 1))
                    pe.wait_ge(*k2_made.after(d, 1))
                    for j in range(2):
                        nb = 2 * n + j
                        last = nc.tensor.matmul(ps[:, j, :], q2[:, nb * P:nb * P + P], k2[:, :], start=True, stop=True)
                elif kind == "t2":
                    pe.wait_ge(*probs2_made.after(d, 1))
                    for j in range(2):
                        for nb in range(KB):
                            mb = 2 * n + j
                            last = nc.tensor.transpose(ps[:, j, nb * P:nb * P + P],
                                                       probs2[:, nb, mb * P:mb * P + P], ident[:, :])
                elif kind == "o2":
                    pe.wait_ge(*probs2T_made.after(d, 2))
                    pe.wait_ge(*v2_made.after(d, 2))
                    for mb in range(KB):
                        last = nc.tensor.matmul(ps[:, 0, :], values2[:, mb, n * P:n * P + P], probs2T[:, mb, :],
                                                start=(mb == 0), stop=(mb == KB - 1))
                last.then_inc(made[kind].sem, 1)

            def scores(b, p, t):
                sub, i = divmod(t, GROUP)
                head, kp = GROUP * (sub // 2) + i, sub % 2
                ps = claim(b, "st", 0, t)
                if t == 0:
                    pe.wait_ge(*shift_in[0].after(b, 16))
                if t == 16:
                    pe.wait_ge(*shift_in[1].after(b, 16))
                for j in range(2):
                    kb = 2 * kp + j
                    last = nc.tensor.matmul(ps[:, j, :], k_stack[p][0:ROWS, head, kb * P:kb * P + P],
                                            q_stack[p][0:ROWS, head, :], start=True, stop=True)
                last.then_inc(made["st"].sem, 1)

            def maxima(b, o, t):
                head, qp = divmod(t, 2)
                ps = claim(b, "mx", 1, t)
                if t == 0:
                    pe.wait_ge(*stack_in[0].after(b + 2, 0))
                    pe.wait_ge(*maskrow_in[0].after(b + 2, 0))
                if t == 16:
                    pe.wait_ge(*stack_in[1].after(b + 2, 0))
                    pe.wait_ge(*maskrow_in[1].after(b + 2, 0))
                for j in range(2):
                    qb = 2 * qp + j
                    last = nc.tensor.matmul(ps[:, j, :], q_stack[o][0:ROW_MAX, head, qb * P:qb * P + P],
                                            k_stack[o][0:ROW_MAX, head, :], start=True, stop=True)
                last.then_inc(made["mx"].sem, 1)

            def attend(d, p, sub, quad):
                g, kp = divmod(sub, 2)
                if quad == 0:
                    pe.wait_ge(*exp_done.after(d, GROUP * sub + GROUP))
                    if kp == 0:
                        pe.wait_ge(*att_copied.after(d, g))
                    if sub == 0:
                        pe.wait_ge(*v_squared.after(d, 2))
                if quad == 2:
                    if sub == 0:
                        pe.wait_ge(*den_copied.after(d, 0))
                    pe.wait_ge(*pair_done.after(d, GROUP * sub + GROUP))
                for i in range(GROUP):
                    rows_ = slice(32 * i, 32 * i + 32)
                    if quad < 2:
                        kb = 2 * kp + quad
                        last = nc.tensor.matmul(att[rows_, :], values[p][:, kb, GROUP * g + i, :],
                                                probs[sub % 2][:, i, quad, :], start=(kb == 0), stop=(kb == KB - 1))
                    else:
                        last = nc.tensor.matmul(den[rows_, :], pick[:, g, :], pairs[sub % 2][:, i, :],
                                                start=(sub == 0), stop=(sub == SUBS - 1))
                if quad == 1:
                    last.then_inc(att_done.sem, 1)
                if quad == 2:
                    last.then_inc(den_done.sem, 1)

            def body(b, p):
                for t in range(STEPS):
                    sub, quad = t // GROUP - 1, t % GROUP
                    if exists(b):
                        scores(b, p, t)
                    if quad < 3:
                        if sub < 0 and exists(b - 1):
                            attend(b - 1, 1 - p, SUBS - 1, quad)
                        if sub >= 0 and exists(b):
                            attend(b, p, sub, quad)
                    if exists(b + 1):
                        maxima(b, 1 - p, t)
                    for kind, off, n in FILLERS.get(t, []):
                        if exists(b + off):
                            filler(b, kind, off, n)

            iterations(pe, body)

        @block.scalar
        def _(act):
            act.wait_ge(maskrow_out, 16)

            def exp(b, t):
                sub, i = divmod(t, GROUP)
                if i == 0:
                    act.wait_ge(*att_done.after(b, sub - 1))
                    act.wait_ge(*pair_done.after(b, GROUP * (sub - 1)))
                act.wait_ge(*made["st"].after(b, t + 1))
                nc.scalar.activation(probs[sub % 2][:, i, :, :], slot("st", 0, t), ACT.Exp, scale=SCALE)\
                    .then_inc(exp_done.sem, 1)

            def rows(dram, d):
                return dram[index(d)].rearrange("(c p) t -> p c t", p=P)

            def load_maskrow(d, p, half):
                act.wait_ge(*made["st"].after(d - 2, 16 * half + 16))
                act.wait_ge(*maskrow_in[half].after(d, 0))
                act.dma_start(k_stack[p][ROW_MASK:ROW_MASK + 1, half * HALF:(half + 1) * HALF, :],
                              maskrow_dram[bass.ds(index(d), 1), half * HALF * T:(half + 1) * HALF * T]
                              .rearrange("o (h t) -> o h t", t=T)).then_inc(maskrow_in[half].sem, 16)

            def loads(b, p, t):
                if t == 0 and exists(b + 1):
                    load_maskrow(b + 1, 1 - p, 1)
                if t == 4 and exists(b - 1):
                    if exists(b + 2):
                        act.wait_ge(*made["q"].after(b + 2, 2))
                    act.dma_start(xs[:, :, :], rows(x_in, b - 1)).then_inc(xr_in.sem, 16)
                    act.dma_start(mask_b8[:, :], mask_in[index(b - 1), :].partition_broadcast(P)).then_inc(mask_in_.sem, 16)
                if t == 10 and exists(b + 3):
                    act.wait_ge(*made["k"].after(b + 2, 2))
                    act.dma_start(ctx_k[:, :, :], rows(ctx_in, b + 3)).then_inc(ctxk_in.sem, 16)
                if t == 11 and exists(b - 1):
                    if exists(b + 1):
                        act.wait_ge(*made["v"].after(b + 1, 1))
                    act.dma_start(ctx_v[:, :, :], rows(ctx_in, b - 1)).then_inc(ctx1_in.sem, 16)
                if t == 18 and exists(b + 3):
                    act.wait_ge(*x_scaled.after(b - 1, 2))
                    act.dma_start(xs[:, :, :], rows(x_in, b + 3)).then_inc(xq_in.sem, 16)
                if t == 17 and exists(b + 2):
                    load_maskrow(b + 2, p, 0)
                if t == 20 and exists(b + 2):
                    if exists(b + 1):
                        act.wait_ge(*made["v"].after(b + 1, 1))
                    act.wait_ge(*made["v2"].after(b - 1, 2))
                    act.dma_start(ctx_v[:, :, :], rows(ctx_in, b + 2)).then_inc(ctxv_in.sem, 16)
                if t == 5 and exists(b - 2):
                    act.wait_ge(*result_made.after(b - 2, 2))
                    act.dma_start(rows(out, b - 2), x1[:, :, :]).then_inc(result_out.sem, 16)

            def copy_moments(d, g):
                act.wait_ge(*att_done.after(d, 2 * g + 2))
                act.wait_ge(*moments_in[g % 2].after(d, 16 * 2 * GROUP * (g // 2)))
                nc.scalar.activation(raw[g % 2][:, :], att[:, :], ACT.Copy).then_inc(att_copied.sem, 1)

            def part_2(n, d, half):
                act.wait_ge(*rest_made[n].after(d, half + 1))
                nc.scalar.activation(split[:, half, 1, :], rest[:, :], ACT.Copy).then_inc(part2[n].sem, 1)

            act.wait_ge(consts, 4)
            act.wait_ge(ones_made, ONES)
            act.dma_start(xs[:, :, :], rows(x_in, 0)).then_inc(xq_in.sem, 16)
            act.dma_start(ctx_k[:, :, :], rows(ctx_in, 0)).then_inc(ctxk_in.sem, 16)

            def body(b, p):
                d = b - 1
                for t in range(STEPS):
                    if exists(b):
                        exp(b, t)
                    loads(b, p, t)
                    if t in (1, 3) and exists(b + 2):
                        part_2(0, b + 2, t // 2)
                    if t in (7, 9) and exists(b + 2):
                        part_2(1, b + 2, t // 2 - 3)
                    if t in (10, 18, 26) and exists(b):
                        copy_moments(b, t // 8 - 1)
                    if t == 2 and exists(d):
                        copy_moments(d, 3)
                    if not exists(d):
                        continue
                    if t == 3:
                        act.wait_ge(*den_done.after(d, SUBS))
                        act.wait_ge(*inv_out.after(d, 0))
                        nc.scalar.activation(inv_rows[:, :], den[:, :], ACT.Copy).then_inc(den_copied.sem, 1)
                    if t == 6:
                        act.wait_ge(*mask_in_.after(d, 16))
                        nc.scalar.activation(mask_b[:, :], mask_b8[:, :], ACT.Copy).then_inc(mask_ready.sem, 1)
                    if t in (8, 9):
                        half = t - 8
                        act.wait_ge(*x_masked.after(d, half + 1))
                        if half == 0:
                            act.wait_ge(*made["o2"].after(d - 1, 2))
                        nc.scalar.activation(square[:, 2 + half, :], xs[:, half, :], ACT.Square,
                                             accum_out=stats[:, 4 + half:5 + half]).then_inc(x_sumsq.sem, 1)
                    if t == 12:
                        act.wait_ge(*mean_made.after(d, 2))
                        nc.scalar.activation(square[:, 0:CH, :], mean[:, :, :], ACT.Square).then_inc(mean_squared.sem, 1)
                    if t == 16:
                        act.wait_ge(*stat_steps.after(d, 5))
                        nc.scalar.activation(spread[:, :], stats[:, 10:12], ACT.Sqrt).then_inc(spread_done.sem, 1)
                        act.wait_ge(*var_clamped.after(d, 1))
                        nc.scalar.activation(ex2[:, :, :], ex2[:, :, :], ACT.Sqrt).then_inc(std_done.sem, 1)
                    if t in (23, 24):
                        for nb in range(2 * (t - 23), 2 * (t - 23) + 2):
                            if nb % 2 == 0:
                                act.wait_ge(*max2_done.after(d, nb // 2 + 1))
                            if nb == 0:
                                act.wait_ge(*made["t2"].after(d - 1, 2))
                            nc.scalar.activation(probs2[:, nb, :], slot("s2", -1, nb // 2)[:, nb % 2, :], ACT.Exp,
                                                 bias=stats2[:, 0, nb:nb + 1], accum_out=stats2[:, 1, nb:nb + 1])\
                                .then_inc(exp2_done.sem, 1)
                    if t == 26:
                        act.wait_ge(*sum2_inv.after(d, 1))
                        for nb in range(KB):
                            last = nc.scalar.activation(probs2[:, nb, :], probs2[:, nb, :], ACT.Copy,
                                                        scale=stats2[:, 2, nb:nb + 1])
                        last.then_inc(probs2_made.sem, 1)
                    if t == 28:
                        for n in range(2):
                            act.wait_ge(*made["t2"].after(d, n + 1))
                            nc.scalar.activation(probs2T[:, 2 * n:2 * n + 2, :], slot("t2", -1, n), ACT.Copy)\
                                .then_inc(probs2T_made.sem, 1)

            iterations(act, body)
            act.wait_ge(*result_out.after(B, 0))

        @block.gpsimd
        def _(pool):
            nc.gpsimd.memset(ident[:, :], 0.0).then_inc(consts, 1)
            pool.wait_ge(consts, 1)
            nc.gpsimd.affine_select(out=ident[:, :], in_=ident[:, :], compare_op=ALU.not_equal, fill=1.0, base=0,
                                    pattern=[[-1, P]], channel_multiplier=1).then_inc(consts, 1)
            for n, stack in enumerate(q_stack):
                pool.wait_ge(consts, 2 + n)
                nc.gpsimd.memset(stack[ROW_MASK:P, :, :].bitcast(fp32), TWO_BF16_ONES).then_inc(consts, 1)

            def part_3(n, d, half):
                pool.wait_ge(*part2[n].after(d, half + 1))
                nc.gpsimd.tensor_tensor(out=split[:, half, 2, :], in0=rest[:, :], in1=split[:, half, 1, :],
                                        op=ALU.subtract).then_inc(part3[n].sem, 1)

            def pair(b, t):
                sub, i = divmod(t, GROUP)
                if i == 0:
                    pool.wait_ge(*den_done.after(b, sub - 1))
                pool.wait_ge(*exp_done.after(b, t + 1))
                nc.gpsimd.tensor_tensor(out=pairs[sub % 2][:, i, :], in0=probs[sub % 2][:, i, 0, :],
                                        in1=probs[sub % 2][:, i, 1, :], op=ALU.add).then_inc(pair_done.sem, 1)

            def body(b, p):
                d = b - 1
                for t in range(STEPS):
                    if exists(b):
                        pair(b, t)
                    if t in (1, 3) and exists(b + 2):
                        part_3(0, b + 2, t // 2)
                    if t in (7, 9) and exists(b + 2):
                        part_3(1, b + 2, t // 2 - 3)
                    if t in (15, 16) and exists(b + 1):
                        half = slice(HEADS * 2 * (t - 15), HEADS * 2 * (t - 14))
                        pool.wait_ge(*v_biased.after(b + 1, 1))
                        v = values[1 - p][:, :, :, :].rearrange("p k h e -> p (k h) e")
                        nc.gpsimd.tensor_tensor(out=v[:, half, D:2 * D], in0=v[:, half, 0:D], in1=v[:, half, 0:D],
                                                op=ALU.mult).then_inc(v_squared.sem, 1)
                    if not exists(d):
                        continue
                    if t in (6, 8):
                        half = t // 2 - 3
                        if half == 0:
                            pool.wait_ge(*mask_ready.after(d, 1))
                            pool.wait_ge(*xr_in.after(d, 16))
                        nc.gpsimd.tensor_tensor(out=xs[:, half, :], in0=xs[:, half, :], in1=mask_b[:, :],
                                                op=ALU.mult).then_inc(x_masked.sem, 1)
                    if t in (10, 11):
                        half = t - 10
                        if half == 0:
                            pool.wait_ge(*moments_in[0].after(d + 1, 0))
                            pool.wait_ge(*moments_in[1].after(d + 1, 0))
                            pool.wait_ge(*inv_in.after(d, 16 * CH))
                        nc.gpsimd.tensor_tensor(out=mean[:, half, :], in0=mean[:, half, :], in1=inv_den[:, half, :],
                                                op=ALU.mult).then_inc(mean_made.sem, 1)
                    if t in (13, 14):
                        half = t - 13
                        if half == 0:
                            pool.wait_ge(*mean_squared.after(d, 1))
                            pool.wait_ge(*ex2_made.after(d, 2))
                        nc.gpsimd.tensor_tensor(out=ex2[:, half, :], in0=ex2[:, half, :], in1=square[:, half, :],
                                                op=ALU.subtract).then_inc(var_made.sem, 1)
                    if t in (19, 20):
                        half = t - 19
                        pool.wait_ge(*x_shifted.after(d, half + 1))
                        nc.gpsimd.tensor_tensor(out=x1[:, half, :], in0=x1[:, half, :], in1=mask_b[:, :],
                                                op=ALU.mult).then_inc(x1_made.sem, 1)

            iterations(pool, body)

        @block.vector
        def _(dve):
            nc.vector.memset(pick[:, :, :], 0.0).then_inc(pick_cleared, 1)
            dve.wait_ge(pick_cleared, 1)
            for g in range(SUBS // 2):
                nc.vector.memset(pick[:, g, :].rearrange("p (k j) -> p j k", j=SUBS // 2)[:, g, :], 1.0)\
                    .then_inc(ones_made, 1)
            for stack in k_stack:
                nc.vector.memset(stack[ROW_MASK:P, :, :].bitcast(fp32), TWO_BF16_ONES).then_inc(ones_made, 1)
            dve.wait_ge(weights_in, 16 * 13)
            nc.vector.tensor_scalar(mask_f, mask_u8[:, :], 1.0, MASKED, ALU.subtract, ALU.mult)\
                .then_inc(mask_scaled, 1)
            dve.wait_ge(mask_scaled, 1)
            for h in range(HEADS):
                nc.vector.tensor_copy(maskrow[:, h * T:h * T + T], mask_f).then_inc(maskrow_made, 1)
            dve.wait_ge(maskrow_out, 16)

            def split_first(n, kind, d, half, bias):
                ps = slot(kind, 2, half)[:, 0, :]
                dve.wait_ge(*made[kind].after(d, half + 1))
                if half == 0:
                    if n == 0:
                        dve.wait_ge(*parts_out[1].after(d, 0))
                        dve.wait_ge(*part3[1].after(d, 0))
                    else:
                        dve.wait_ge(*parts_out[0].after(d, 32))
                        dve.wait_ge(*part3[0].after(d, 2))
                nc.vector.tensor_scalar(split[:, half, 0, :], ps, bias[:, half:half + 1], None, ALU.add)\
                    .then_inc(part1[n].sem, 1)
                dve.wait_ge(*part1[n].after(d, half + 1))
                if half == 1:
                    dve.wait_ge(*part3[n].after(d, 1))
                nc.vector.scalar_tensor_tensor(out=rest[:, :], in0=ps, scalar=bias[:, half:half + 1],
                                               in1=split[:, half, 0, :], op0=ALU.add, op1=ALU.subtract)\
                    .then_inc(rest_made[n].sem, 1)

            def add_value_bias(d, dst):
                dve.wait_ge(*made["v"].after(d, 1))
                ps = slot("v", 1, 0)
                for kb in range(KB):
                    last = nc.vector.tensor_tensor(
                        out=dst[:, kb, :, 0:D],
                        in0=ps[:, kb // 2, (kb % 2) * C:(kb % 2) * C + C].rearrange("p (h d) -> p h d", d=D),
                        in1=bv_sb[:, :].rearrange("p (h d) -> p h d", d=D), op=ALU.add)
                last.then_inc(v_biased.sem, 1)

            def add_value2_bias(d, n):
                dve.wait_ge(*made["v2"].after(d, n + 1))
                if n == 0:
                    dve.wait_ge(*made["o2"].after(d - 1, 2))
                nc.vector.tensor_tensor(out=values2[:, 2 * n:2 * n + 2, :],
                                        in0=slot("v2", -1, n)[:, 0, :].rearrange("p (k c) -> p k c", k=2),
                                        in1=b1v_sb[:, :].unsqueeze(1).to_broadcast([P, 2, C]),
                                        op=ALU.add).then_inc(v2_made.sem, 1)

            def shift_rows(d, off, half):
                ps = slot("shift", off, half)[0:32, 0, 0:P]
                dve.wait_ge(*made["shift"].after(d, half + 1))
                dve.wait_ge(*shift_out[1 - half].after(d + half - 1, 16))
                nc.vector.tensor_scalar(neg_max[:, 0, :], ps, -1.0, None, ALU.mult).then_inc(neg1.sem, 1)
                dve.wait_ge(*neg1.after(d, half + 1))
                nc.vector.scalar_tensor_tensor(out=neg_rest[:, :], in0=ps, scalar=-1.0, in1=neg_max[:, 0, :],
                                               op0=ALU.mult, op1=ALU.subtract).then_inc(shift_rest.sem, 1)
                dve.wait_ge(*shift_rest.after(d, half + 1))
                nc.vector.tensor_copy(neg_max[:, 1, :], neg_rest[:, :]).then_inc(neg2.sem, 1)
                dve.wait_ge(*neg2.after(d, half + 1))
                nc.vector.tensor_tensor(out=neg_max[:, 2, :], in0=neg_rest[:, :], in1=neg_max[:, 1, :],
                                        op=ALU.subtract).then_inc(neg3.sem, 1)

            def invert(d, j):
                cols = slice(j * P, j * P + P)
                if j == 0:
                    dve.wait_ge(*den_copied.after(d, 1))
                nc.vector.reciprocal(inv_rows[:, cols], inv_rows[:, cols]).then_inc(inv_made.sem, 1)

            def instance_stats(d):
                s = stats
                dve.wait_ge(*n_valid.after(d, 1))
                nc.vector.reciprocal(s[:, 1:2], s[:, 0:1]).then_inc(stat_steps.sem, 1)
                dve.wait_ge(*stat_steps.after(d, 1))
                dve.wait_ge(*x_sum.after(d, 1))
                nc.vector.tensor_scalar(s[:, 6:8], s[:, 2:4], s[:, 1:2], None, ALU.mult).then_inc(stat_steps.sem, 1)
                dve.wait_ge(*x_sumsq.after(d, 2))
                dve.wait_ge(*stat_steps.after(d, 2))
                nc.vector.tensor_tensor(out=s[:, 8:10], in0=s[:, 6:8], in1=s[:, 6:8], op=ALU.mult)\
                    .then_inc(stat_steps.sem, 1)
                dve.wait_ge(*stat_steps.after(d, 3))
                nc.vector.scalar_tensor_tensor(out=s[:, 10:12], in0=s[:, 4:6], scalar=s[:, 1:2], in1=s[:, 8:10],
                                               op0=ALU.mult, op1=ALU.subtract).then_inc(stat_steps.sem, 1)
                dve.wait_ge(*stat_steps.after(d, 4))
                nc.vector.tensor_scalar(s[:, 10:12], s[:, 10:12], 0.0, EPS, ALU.max, ALU.add)\
                    .then_inc(stat_steps.sem, 1)

            def split_q2(d):
                ps = slot("q2", -1, 0)[:, 0, :]
                dve.wait_ge(*made["q2"].after(d, 1))
                dve.wait_ge(*made["s2"].after(d - 1, 2))
                nc.vector.tensor_scalar(q2[:, :], ps, b1q_sb[:, :], None, ALU.add).then_inc(q2_hi.sem, 1)
                dve.wait_ge(*q2_hi.after(d, 1))
                nc.vector.scalar_tensor_tensor(out=q2[64:128, :], in0=ps[64:128], scalar=b1q_sb[64:128, :],
                                               in1=q2[64:128, :].bitcast(fp32), op0=ALU.add, op1=ALU.subtract)\
                    .then_inc(q2_made.sem, 1)

            def split_k2(d):
                ps = slot("k2", -1, 0)[:, 0, :]
                dve.wait_ge(*made["k2"].after(d, 1))
                dve.wait_ge(*made["s2"].after(d - 1, 2))
                nc.vector.tensor_scalar(k2[:, :], ps, b1k_sb[:, :], None, ALU.add).then_inc(k2_hi.sem, 1)
                dve.wait_ge(*k2_hi.after(d, 1))
                for lo in (32, 96):
                    last = nc.vector.scalar_tensor_tensor(
                        out=k2[lo:lo + 32, :], in0=ps[lo:lo + 32], scalar=b1k_sb[lo:lo + 32, :],
                        in1=k2[lo:lo + 32, :].bitcast(fp32), op0=ALU.add, op1=ALU.subtract)
                    last.then_inc((k2_hi if lo == 32 else k2_made).sem, 1)

            def body(b, p):
                d = b - 1
                for t in range(STEPS):
                    if exists(b + 1):
                        dve.wait_ge(*made["mx"].after(b + 1, t + 1))
                        if t % 16 == 0:
                            dve.wait_ge(*made["shift"].after(b, t // 16 + 1))
                        nc.vector.reduce_max(row_max[:, t // 16, 2 * (t % 16):2 * (t % 16) + 2], slot("mx", 1, t),
                                             axis=AX.X).then_inc(max_done.sem, 1)
                    if t in (0, 2) and exists(b + 2):
                        split_first(0, "q", b + 2, t // 2, bq_sb)
                    if t == 1 and exists(b):
                        shift_rows(b, 0, 1)
                    if t in (1, 3) and exists(b - 2):
                        n = t // 2
                        dve.wait_ge(*made["o2"].after(b - 2, n + 1))
                        nc.vector.tensor_tensor(out=x1[:, n, :], in0=slot("o2", -2, n)[:, 0, :], in1=x1[:, n, :],
                                                op=ALU.add).then_inc(result_made.sem, 1)
                    if t in (6, 8) and exists(b + 2):
                        split_first(1, "k", b + 2, t // 2 - 3, bk_sb)
                    if t == 9 and exists(b + 1):
                        dve.wait_ge(*att_done.after(b - 1, SUBS))
                        add_value_bias(b + 1, values[1 - p])
                    if t == 16 and exists(b + 1):
                        shift_rows(b + 1, 1, 0)
                    if not exists(d):
                        continue
                    if t in (4, 5):
                        invert(d, 2 * (t - 4))
                        invert(d, 2 * (t - 4) + 1)
                    if t == 7:
                        dve.wait_ge(*mask_ready.after(d, 1))
                        nc.vector.reduce_sum(stats[:, 0:1], mask_b[:, :], axis=AX.X).then_inc(n_valid.sem, 1)
                    if t == 10:
                        dve.wait_ge(*moments_in[0].after(d + 1, 0))
                        dve.wait_ge(*moments_in[1].after(d + 1, 0))
                        dve.wait_ge(*inv_in.after(d, 16 * CH))
                        for half in range(CH):
                            nc.vector.tensor_tensor(out=ex2[:, half, :], in0=ex2[:, half, :], in1=inv_den[:, half, :],
                                                    op=ALU.mult).then_inc(ex2_made.sem, 1)
                    if t == 11:
                        dve.wait_ge(*x_masked.after(d, 2))
                        nc.vector.reduce_sum(stats[:, 2:4], xs[:, :, :], axis=AX.X).then_inc(x_sum.sem, 1)
                    if t == 12:
                        instance_stats(d)
                    if t == 13:
                        split_k2(d)
                    if t == 15:
                        dve.wait_ge(*var_made.after(d, 2))
                        nc.vector.tensor_scalar(ex2[:, :, :], ex2[:, :, :], 0.0, None, ALU.max)\
                            .then_inc(var_clamped.sem, 1)
                        add_value2_bias(d, 0)
                    if t == 17:
                        dve.wait_ge(*spread_done.after(d, 1))
                        nc.vector.reciprocal(stats[:, 12:14], spread[:, :]).then_inc(stat_steps.sem, 1)
                        dve.wait_ge(*std_done.after(d, 1))
                        dve.wait_ge(*mean_made.after(d, 2))
                        dve.wait_ge(*ex2_made.after(d, 2))
                        for half in range(CH):
                            nc.vector.scalar_tensor_tensor(out=x1[:, half, :], in0=xs[:, half, :],
                                                           scalar=stats[:, 6 + half:7 + half], in1=ex2[:, half, :],
                                                           op0=ALU.subtract, op1=ALU.mult).then_inc(x_scaled.sem, 1)
                    if t == 18:
                        dve.wait_ge(*stat_steps.after(d, 6))
                        for half in range(CH):
                            dve.wait_ge(*x_scaled.after(d, half + 1))
                            nc.vector.scalar_tensor_tensor(out=x1[:, half, :], in0=x1[:, half, :],
                                                           scalar=stats[:, 12 + half:13 + half], in1=mean[:, half, :],
                                                           op0=ALU.mult, op1=ALU.add).then_inc(x_shifted.sem, 1)
                    if t == 19:
                        add_value2_bias(d, 1)
                    if t == 21:
                        split_q2(d)
                    if t in (23, 24):
                        n = t - 23
                        dve.wait_ge(*made["s2"].after(d, n + 1))
                        nc.vector.reduce_max(stats2[:, 0, 2 * n:2 * n + 2], slot("s2", -1, n), axis=AX.X,
                                             negate=True).then_inc(max2_done.sem, 1)
                    if t == 25:
                        dve.wait_ge(*exp2_done.after(d, KB))
                        nc.vector.reciprocal(stats2[:, 2, :], stats2[:, 1, :]).then_inc(sum2_inv.sem, 1)

            iterations(dve, body)


def kernel(x, ctx_2048, mask_Bx1x2048_bf1, L0_xattn_Wq, L0_xattn_bq, L0_xattn_Wk, L0_xattn_bk, L0_xattn_Wv,
           L0_xattn_bv, L1_xattn_Wq, L1_xattn_bq, L1_xattn_Wk, L1_xattn_bk, L1_xattn_Wv, L1_xattn_bv):
    import numpy as np
    import concourse.bacc as bacc
    from concourse import mybir
    from concourse.bass_utils import run_bass_kernel_spmd

    def T_(w):
        return np.ascontiguousarray(np.asarray(w).T)

    def halves(v):
        return np.ascontiguousarray(np.asarray(v).reshape(2, 128).T)

    arrays = dict(
        x=np.ascontiguousarray(x), ctx=np.ascontiguousarray(ctx_2048),
        mask=np.ascontiguousarray(mask_Bx1x2048_bf1).reshape(16, 512).view(np.uint8),
        wqT=T_(L0_xattn_Wq), bq=halves(L0_xattn_bq), wkT=T_(L0_xattn_Wk), bk=halves(L0_xattn_bk),
        wvT=T_(L0_xattn_Wv), bv=np.ascontiguousarray(L0_xattn_bv),
        w1qT=np.tile(T_(L1_xattn_Wq), (1, 4)), b1q=np.tile(np.asarray(L1_xattn_bq), 4).reshape(128, 1),
        w1kT=np.tile(T_(L1_xattn_Wk), (1, 4)), b1k=np.tile(np.asarray(L1_xattn_bk), 4).reshape(128, 1),
        w1vT=T_(L1_xattn_Wv), b1v=np.ascontiguousarray(L1_xattn_bv))
    nc = bacc.Bacc("TRN2", target_bir_lowering=False, num_devices=1)
    args = [nc.dram_tensor(f"{n}_dram", a.shape, mybir.dt.from_np(a.dtype), kind="ExternalInput").ap()
            for n, a in arrays.items()]
    out = nc.dram_tensor("out_dram", (16, 256, 512), mybir.dt.float32, kind="ExternalOutput").ap()
    build(nc, *args, out)
    r = run_bass_kernel_spmd(nc, [{f"{n}_dram": a for n, a in arrays.items()}], core_ids=[0])
    return r.results[0]["out_dram"]
```

```python
import concourse.bass as bass
from concourse import mybir
from contextlib import ExitStack

B, C, T = 16, 256, 512
HEADS, D = 16, 16
D1 = 32
P = 128
CH = C // P
KB = T // P
HALF = HEADS // 2
STEPS = 2 * HEADS
GROUP = 4
SUBS = STEPS // GROUP
PARTS = 3
Q_PARTS = (0, 1, 0, 1, 0, 2)
K_PARTS = (0, 0, 1, 1, 2, 0)
ROW_MASK = D * len(Q_PARTS)
ROW_MAX = ROW_MASK + 1
ROWS = ROW_MAX + PARTS
SCALE = 1.0 / float(D) ** 0.5
MASKED = 3.0e38
TWO_BF16_ONES = 1.0 + 0x3F80 * 2.0 ** -23
EPS = 1e-5
RING = 3

AT = {
    ("q", 0): -69, ("q", 1): -66, ("k", 0): -57, ("k", 1): -44, ("v", 0): -14, ("shift", 0): -10, ("shift", 1): 5,
    ("k2", 0): 42, ("v2", 0): 46, ("v2", 1): 46, ("q2", 0): 55, ("s2", 0): 59, ("s2", 1): 63, ("t2", 0): 66,
    ("t2", 1): 67, ("o2", 0): 70, ("o2", 1): 74,
    "load q": -76, "load k": -75, "load maskrow 0": -47, "load maskrow 1": -29, "load v": -17, "load x": 32,
    "load ctx 1": 19, "mask": 35, "copy den": 37, "x sums 0": 40, "x sums 1": 42, "mean^2": 46, "sqrt": 50,
    "scale 0": 65, "result": 78,
    "v^2 0": -11, "v^2 1": -7, "mask x 0": 37, "mask x 1": 38, "mean 0": 43, "mean 1": 44, "var 0": 47, "var 1": 48,
    "invert": 40, "stats": 44, "ex2": 45, "clamp": 50, "x scale": 51, "x shift": 52, "x mask": 52, "scale 1": 64,
    "store q": -63, "store k": -42, "stack 0": -42, "stack 1": -28, "shift 0": -8, "shift 1": 10, "compact 0": 21,
    "compact 1": 21, "compact 2": 29, "compact 3": 35, "pack den": 36, "spread inv": 41,
}
SUM_LAG = 2
FILLERS = {_t: [(_kind, -(AT[_kind, _n] // STEPS), _n)
                for _kind in ("s2", "t2", "k2", "q2", "o2", "shift", "v2", "k", "q", "v") for _n in (0, 1)
                if (_kind, _n) in AT and AT[_kind, _n] % STEPS == _t] for _t in range(STEPS)}
JOBS = []
for _t in range(STEPS):
    JOBS += [("st", 0, _t), ("mx", 1, _t)] + FILLERS[_t]
assert len(JOBS) % RING == 0
OFFSET = {(_kind, _n): _off for _kind, _off, _n in JOBS}
FIRST, LAST = -3, B + 1
LOOP_FROM, LOOP_TO = 3, B - 3

LOOP_I = 8


class Looped:

    def __init__(self, i, c):
        self.i, self.c = i, c

    def __add__(self, n):
        return Looped(self.i, self.c + n)

    def __sub__(self, n):
        return Looped(self.i, self.c - n)

    def times(self, per, n):
        return self.i * (2 * per) + (self.c * per + n)


def index(d):
    return d if isinstance(d, int) else d.times(1, 0)


def exists(d):
    return not isinstance(d, int) or 0 <= d < B


def due(b, t, when):
    if t != when % STEPS:
        return None
    d = b - when // STEPS
    return d if exists(d) else None


def parity(p, when):
    return (p + when // STEPS) % 2


SEQUENCE = [(_kind, _b + _off, _n) for _b in range(FIRST, LAST + 1) for _kind, _off, _n in JOBS if 0 <= _b + _off < B]
_BEFORE_LOOP = sum(0 <= _b + _off < B for _b in range(FIRST, LOOP_FROM) for _, _off, _ in JOBS)
PLACE = {_job: (_i - _BEFORE_LOOP) % RING for _i, _job in enumerate(SEQUENCE)}
assert all(0 <= _b + _off < B for _b in range(LOOP_FROM - 1, LOOP_TO) for _, _off, _ in JOBS)


def ring_place(kind, d, n):
    if isinstance(d, int):
        return PLACE[kind, d, n]
    return JOBS.index((kind, OFFSET[kind, n], n)) % RING


def ring_before(b, kind, off, n):
    if isinstance(b, int):
        at = SEQUENCE.index((kind, b + off, n)) - RING
        return SEQUENCE[at] if at >= 0 else None
    at = JOBS.index((kind, off, n)) - RING
    k, o, m = JOBS[at]
    return k, (b + o if at >= 0 else b - 1 + o), m


def build(nc, x_in, ctx_in, mask_in, wqT, bq, wkT, bk, wvT, bv, w1qT, b1q, w1kT, b1k, w1vT, b1v, out):
    fp32, bf16, fp32r = mybir.dt.float32, mybir.dt.bfloat16, mybir.dt.float32r
    ALU, ACT, AX = mybir.AluOpType, mybir.ActivationFunctionType, mybir.AxisListType

    parts_dram = [[nc.dram_tensor(f"parts_{n}{p}", (PARTS, C, T), bf16, kind="Internal").ap()
                   for p in range(2)] for n in "qk"]
    shift_dram = [[nc.dram_tensor(f"shift_{h}{p}", (PARTS, HALF * KB, P), bf16, kind="Internal").ap()
                   for p in range(2)] for h in range(2)]
    den_dram = nc.dram_tensor("den_dram", (HEADS, T), fp32, kind="Internal").ap()
    inv_dram = nc.dram_tensor("inv_dram", (HEADS, T), fp32, kind="Internal").ap()
    maskrow_dram = nc.dram_tensor("maskrow", (B, HEADS * T), bf16, kind="Internal").ap()

    ctx = ExitStack()
    with ctx:
        def sb(name, shape, dt):
            return ctx.enter_context(nc.sbuf_tensor(name, shape, dt))

        def sem(name):
            return ctx.enter_context(nc.semaphore(name))

        class Tally:

            def __init__(self, name, per):
                self.sem, self.per = sem(name), per

            def after(self, d, n):
                return self.sem, (max(d * self.per + n, 0) if isinstance(d, int) else d.times(self.per, n))

        turns = sem("turns")

        wq_sb, wk_sb = sb("wq_sb", [P, CH, C], fp32), sb("wk_sb", [P, CH, C], fp32)
        wv_sb, w1v_sb = sb("wv_sb", [P, CH, C], fp32), sb("w1v_sb", [P, CH, C], fp32)
        w1q_sb, w1k_sb = sb("w1q_sb", [P, CH, P], fp32), sb("w1k_sb", [P, CH, P], fp32)
        bq_sb, bk_sb = sb("bq_sb", [P, CH], fp32), sb("bk_sb", [P, CH], fp32)
        b1q_sb, b1k_sb = sb("b1q_sb", [P, 1], fp32), sb("b1k_sb", [P, 1], fp32)
        bv_sb, b1v_sb = sb("bv_sb", [P, C], fp32), sb("b1v_sb", [P, C], fp32)
        ident, pick = sb("ident", [P, P], fp32), sb("pick", [P, SUBS // 2, 32], fp32)
        xs, ctx_k = sb("xs", [P, CH, T], fp32), sb("ctx_k", [P, CH, T], fp32)
        ctx_v = sb("ctx_v", [P, CH, T], fp32)
        split, rest = sb("split", [P, CH, PARTS, T], bf16), sb("rest", [P, T], fp32)
        q_stack = [sb(f"q_stack{p}", [P, HEADS, T], bf16) for p in range(2)]
        k_stack = [sb(f"k_stack{p}", [P, HEADS, T], bf16) for p in range(2)]
        row_max = sb("row_max", [P, 2, HALF * KB], fp32)
        neg_max, neg_rest = sb("neg_max", [32, PARTS, P], bf16), sb("neg_rest", [32, P], fp32)
        values = [sb(f"values{p}", [P, KB, HEADS, 2 * D], fp32) for p in range(2)]
        probs = [sb(f"probs{p}", [P, GROUP, 2, T], fp32) for p in range(2)]
        pairs = [sb(f"pairs{p}", [P, GROUP, T], fp32) for p in range(2)]
        raw = [sb(f"raw{p}", [P, T], fp32) for p in range(2)]
        den_rows, dens = sb("den_rows", [P, T], fp32), sb("dens", [P, HEADS * T // P], fp32)
        mean, ex2 = sb("mean", [P, CH, T], fp32), sb("ex2", [P, CH, T], fp32)
        mask_b8, mask_b = sb("mask_b8", [P, T], mybir.dt.uint8), sb("mask_b", [P, T], fp32)
        stats, spread = sb("stats", [P, 16], fp32), sb("spread", [P, CH], fp32)
        x1 = sb("x1", [P, CH, T], fp32)
        q2, k2 = sb("q2", [P, T], fp32r), sb("k2", [P, T], fp32r)
        values2 = sb("values2", [P, KB, C], fp32)
        probs2, probs2T = sb("probs2", [P, KB, T], fp32), sb("probs2T", [P, KB, T], fp32)
        stats2 = sb("stats2", [P, 3, KB], fp32)
        mask_u8 = raw[0][0:B, 0:T // 4].bitcast(mybir.dt.uint8)
        mask_f = probs[1][0:B, 0, 0, :]
        maskrow = probs[0][0:B, :, :, :].rearrange("p a b t -> p (a b t)").bitcast(bf16)[:, 0:HEADS * T]
        inv_den, square = probs2[:, 0:CH, :], probs2[:, CH:2 * CH, :]

        ring = ctx.enter_context(nc.psum_tensor("ring", [P, RING, 2, T], fp32))
        att = ctx.enter_context(nc.psum_tensor("att", [P, T], fp32))
        den = ctx.enter_context(nc.psum_tensor("den", [P, T], fp32))

        pick_cleared = sem("pick_cleared")
        ONES = SUBS // 2 + len(k_stack)
        wq_in, wk_in, mask_u8_in = sem("wq_in"), sem("wk_in"), sem("mask_u8_in")
        WEIGHTS = 16 * 8
        weights_in, consts, ones_made, mask_scaled = sem("weights_in"), sem("consts"), sem("ones_made"), sem("mask_scaled")
        maskrow_made, maskrow_out = sem("maskrow_made"), sem("maskrow_out")
        xq_in, xr_in = Tally("xq_in", 16), Tally("xr_in", 16)
        ctxk_in, ctxv_in, ctx1_in = Tally("ctxk_in", 16), Tally("ctxv_in", 16), Tally("ctx1_in", 16)
        mask_in_ = Tally("mask_in_", 16)
        parts_out = [Tally(f"parts_out_{n}", 32) for n in "qk"]
        stack_in = [Tally(f"stack_in{h}", 16 * 2 * len(Q_PARTS)) for h in range(2)]
        maskrow_in = [Tally(f"maskrow_in{h}", 16) for h in range(2)]
        shift_out = [Tally(f"shift_out{h}", 16) for h in range(2)]
        shift_in = [Tally(f"shift_in{h}", 16) for h in range(2)]
        moments_in = [Tally(f"moments_in{n}", 16 * HEADS) for n in range(2)]
        den_out, den_in = Tally("den_out", 16 * GROUP), Tally("den_in", 16)
        inv_out, inv_in = Tally("inv_out", 16), Tally("inv_in", 16 * CH)
        result_out = Tally("result_out", 16)
        made = {k: Tally(f"made_{k}", n) for k, n in dict(
            st=STEPS, mx=STEPS, q=2, k=2, v=1, shift=2, k2=1, v2=2, q2=1, s2=2, t2=2, o2=2).items()}
        att_done, den_done = Tally("att_done", SUBS), Tally("den_done", SUBS // 2)
        exp_done, max_done = Tally("exp_done", STEPS), Tally("max_done", STEPS)
        rest_made = [Tally(f"rest_made_{n}", 2) for n in "qk"]
        v_biased, shift_rest = Tally("v_biased", 1), Tally("shift_rest", 2)
        k2_made, v2_made, q2_made = Tally("k2_made", 1), Tally("v2_made", 2), Tally("q2_made", 1)
        exp2_done, probs2T_made, result_made = Tally("exp2_done", KB), Tally("probs2T_made", 2), Tally("result_made", 2)
        FREED = dict(st=(exp_done, 1), mx=(max_done, 1), q=(rest_made[0], 1), k=(rest_made[1], 1),
                     v=(v_biased, 1), shift=(shift_rest, 1), k2=(k2_made, 1), v2=(v2_made, 1),
                     q2=(q2_made, 1), s2=(exp2_done, 2), t2=(probs2T_made, 1), o2=(result_made, 1))
        part1 = [Tally(f"part1_{n}", 2) for n in "qk"]
        part2 = [Tally(f"part2_{n}", 2) for n in "qk"]
        part3 = [Tally(f"part3_{n}", 2) for n in "qk"]
        neg1, neg2, neg3 = Tally("neg1", 2), Tally("neg2", 2), Tally("neg3", 2)
        v_squared, pair_done, sum_done = Tally("v_squared", 2), Tally("pair_done", STEPS), Tally("sum_done", HEADS)
        att_copied, den_copied, inv_made = Tally("att_copied", 4), Tally("den_copied", 1), Tally("inv_made", 1)
        mask_ready, x_masked = Tally("mask_ready", 1), Tally("x_masked", 2)
        x_sum, x_sumsq = Tally("x_sum", 2), Tally("x_sumsq", 2)
        stat_steps = Tally("stat_steps", 6)
        spread_done, std_done = Tally("spread_done", 1), Tally("std_done", 1)
        mean_made, ex2_made = Tally("mean_made", 2), Tally("ex2_made", 2)
        mean_squared, var_made, var_clamped = Tally("mean_squared", 1), Tally("var_made", 2), Tally("var_clamped", 1)
        x_scaled, x_shifted, x1_made = Tally("x_scaled", 2), Tally("x_shifted", 2), Tally("x1_made", 2)
        q2_hi, k2_hi = Tally("q2_hi", 1), Tally("k2_hi", 1)
        max2_done, sum2_inv, probs2_made = Tally("max2_done", 2), Tally("sum2_inv", 1), Tally("probs2_made", 2)

        def slot(kind, d, n):
            return ring[:, ring_place(kind, d, n)]

        def iterations(eng, body):
            for b in range(FIRST, LOOP_FROM):
                body(b, b % 2)
            with eng.Fori(LOOP_I, LOOP_I + (LOOP_TO - LOOP_FROM) // 2) as i:
                body(Looped(i, LOOP_FROM - 2 * LOOP_I), LOOP_FROM % 2)
                body(Looped(i, LOOP_FROM + 1 - 2 * LOOP_I), (LOOP_FROM + 1) % 2)
            for b in range(LOOP_TO, LAST + 1):
                body(b, b % 2)

        block = ctx.enter_context(nc.Block())

        @block.sync
        def _(sp):
            for dst, src, into in ((wq_sb, wqT, wq_in), (wk_sb, wkT, wk_in)):
                sp.dma_start(dst[:, :, :], src.rearrange("(c p) o -> p c o", p=P)).then_inc(into, 16)
            for dst, src, into in ((bq_sb, bq, wq_in), (bk_sb, bk, wk_in)):
                sp.dma_start(dst[:, :], src).then_inc(into, 16)
            sp.dma_start(mask_u8[:, :], mask_in).then_inc(mask_u8_in, 16)
            sp.wait_ge(wk_in, 32)
            for dst, src in ((wv_sb, wvT), (w1v_sb, w1vT), (w1q_sb, w1qT), (w1k_sb, w1kT)):
                sp.dma_start(dst[:, :, :], src.rearrange("(c p) o -> p c o", p=P)).then_inc(weights_in, 16)
            for dst, src in ((b1q_sb, b1q), (b1k_sb, b1k)):
                sp.dma_start(dst[:, :], src).then_inc(weights_in, 16)
            for dst, src in ((bv_sb, bv), (b1v_sb, b1v)):
                sp.dma_start(dst[:, :], src.partition_broadcast(P)).then_inc(weights_in, 16)
            sp.wait_ge(consts, 4)
            sp.wait_ge(ones_made, ONES)
            sp.wait_ge(maskrow_made, HEADS)
            sp.dma_start(maskrow_dram, maskrow).then_inc(maskrow_out, 16)
            sp.wait_ge(maskrow_out, 16)

            def load_stack(d, p, half):
                sp.wait_ge(*made["st"].after(d - 2, 16 * half + 16))
                sp.sem_inc(turns, 1)
                sp.wait_ge(*stack_in[half].after(d, 0))
                sp.sem_inc(turns, 1)
                sp.wait_ge(*parts_out[0].after(d, 32))
                sp.sem_inc(turns, 1)
                sp.wait_ge(*parts_out[1].after(d, 32))
                here = slice(half * HALF, half * HALF + HALF)
                for n, (stack, order) in enumerate(((q_stack[p], Q_PARTS), (k_stack[p], K_PARTS))):
                    for j, part in enumerate(order):
                        src = parts_dram[n][p][part, half * P:half * P + P, :]
                        sp.dma_start(stack[D * j:D * j + D, here, :], src.rearrange("(h d) t -> d h t", d=D))\
                            .then_inc(stack_in[half].sem, 16)

            def load_shift(d, p, half):
                sp.wait_ge(*neg3.after(d, half + 1))
                sp.sem_inc(turns, 1)
                sp.wait_ge(*shift_out[half].after(d, 0))
                sp.dma_start(shift_dram[half][p].rearrange("s r i -> r s i"), neg_max[:, :, :])\
                    .then_inc(shift_out[half].sem, 16)
                sp.wait_ge(*shift_out[half].after(d, 16))
                sp.sem_inc(turns, 1)
                sp.wait_ge(*shift_in[half].after(d, 0))
                sp.dma_start(q_stack[p][ROW_MAX:ROWS, half * HALF:(half + 1) * HALF, :],
                             shift_dram[half][p].rearrange("s (h q) i -> s h (q i)", q=KB))\
                    .then_inc(shift_in[half].sem, 16)

            def store_parts(n, d, p):
                for half in range(2):
                    sp.wait_ge(*part3[n].after(d, half + 1))
                    sp.dma_start(parts_dram[n][p][:, half * P:half * P + P, :].rearrange("s p t -> p s t"),
                                 split[:, half, :, :]).then_inc(parts_out[n].sem, 16)

            def compact(d, g):
                sp.wait_ge(*att_copied.after(d, g + 1))
                sp.sem_inc(turns, 1)
                sp.wait_ge(*x_shifted.after(d, 0))
                for i in range(GROUP):
                    head = GROUP * g + i
                    row = D * (head % HALF)
                    for m, dst in enumerate((mean, ex2)):
                        sp.dma_start(dst[row:row + D, head // HALF, :],
                                     raw[g % 2][32 * i + D * m:32 * i + D * m + D, :])\
                            .then_inc(moments_in[g % 2].sem, 16)

            def pack_denominators(d):
                sp.wait_ge(*den_copied.after(d, 1))
                sp.sem_inc(turns, 1)
                sp.wait_ge(*den_out.after(d, 0))
                sp.sem_inc(turns, 1)
                sp.wait_ge(*den_in.after(d, 0))
                for i in range(GROUP):
                    sp.dma_start(den_dram.rearrange("(g i) t -> i g t", i=GROUP)[i],
                                 den_rows[32 * i:32 * i + HEADS // GROUP, :]).then_inc(den_out.sem, 16)
                sp.wait_ge(*den_out.after(d, 16 * GROUP))
                sp.sem_inc(turns, 1)
                sp.wait_ge(*inv_out.after(d, 0))
                sp.dma_start(dens[:, :], den_dram.rearrange("h (c t) -> (h c) t", t=HEADS * T // P))\
                    .then_inc(den_in.sem, 16)

            def spread_inverses(d):
                sp.wait_ge(*inv_made.after(d, 1))
                sp.sem_inc(turns, 1)
                sp.wait_ge(*inv_in.after(d, 0))
                sp.dma_start(inv_dram.rearrange("h (c t) -> (h c) t", t=HEADS * T // P), dens[:, :])\
                    .then_inc(inv_out.sem, 16)
                sp.wait_ge(*inv_out.after(d, 16))
                sp.sem_inc(turns, 1)
                sp.wait_ge(*made["t2"].after(d, 0))
                for half in range(CH):
                    sp.dma_start(inv_den[:, half, :],
                                 inv_dram[half * HALF:half * HALF + HALF, :].unsqueeze(1).to_broadcast([HALF, D, T]))\
                        .then_inc(inv_in.sem, 16)

            def body(b, p):
                for t in range(STEPS):
                    when = AT["store q"]
                    d = due(b, t, when)
                    if d is not None:
                        store_parts(0, d, parity(p, when))
                    when = AT["store k"]
                    d = due(b, t, when)
                    if d is not None:
                        store_parts(1, d, parity(p, when))
                    d = due(b, t, AT["compact 3"])
                    if d is not None:
                        compact(d, 3)
                    d = due(b, t, AT["compact 0"])
                    if d is not None:
                        compact(d, 0)
                    d = due(b, t, AT["compact 1"])
                    if d is not None:
                        compact(d, 1)
                    d = due(b, t, AT["compact 2"])
                    if d is not None:
                        compact(d, 2)
                    d = due(b, t, AT["pack den"])
                    if d is not None:
                        pack_denominators(d)
                    d = due(b, t, AT["spread inv"])
                    if d is not None:
                        spread_inverses(d)
                    when = AT["shift 0"]
                    d = due(b, t, when)
                    if d is not None:
                        load_shift(d, parity(p, when), 0)
                    when = AT["shift 1"]
                    d = due(b, t, when)
                    if d is not None:
                        load_shift(d, parity(p, when), 1)
                    when = AT["stack 0"]
                    d = due(b, t, when)
                    if d is not None:
                        load_stack(d, parity(p, when), 0)
                    when = AT["stack 1"]
                    d = due(b, t, when)
                    if d is not None:
                        load_stack(d, parity(p, when), 1)

            iterations(sp, body)

        @block.tensor
        def _(pe):
            pe.wait_ge(wq_in, 32)

            def claim(b, kind, off, n):
                before = ring_before(b, kind, off, n)
                if before is not None:
                    k, d, m = before
                    tally, per = FREED[k]
                    pe.wait_ge(*tally.after(d, per * (m + 1)))
                return slot(kind, b + off, n)

            def project(dst, w, cols, data, start_stop=True):
                for c in range(CH):
                    last = nc.tensor.matmul(dst, w[:, c, cols], data[:, c, :], start=(c == 0), stop=(c == CH - 1))
                return last

            def project_T(dst, data, w, blocks):
                for j, kb in enumerate(blocks):
                    for c in range(CH):
                        last = nc.tensor.matmul(dst[:, j // 2, (j % 2) * C:(j % 2) * C + C],
                                                data[:, c, kb * P:kb * P + P], w[:, c, :],
                                                start=(c == 0), stop=(c == CH - 1))
                return last

            def filler(b, kind, off, n):
                d = b + off
                ps = claim(b, kind, off, n)
                if kind == "q":
                    pe.wait_ge(*xq_in.after(d, 16))
                    last = project(ps[:, 0, :], wq_sb, slice(n * P, n * P + P), xs)
                elif kind == "k":
                    pe.wait_ge(*ctxk_in.after(d, 16))
                    last = project(ps[:, 0, :], wk_sb, slice(n * P, n * P + P), ctx_k)
                elif kind == "v":
                    pe.wait_ge(*ctxv_in.after(d, 16))
                    last = project_T(ps, ctx_v, wv_sb, range(KB))
                elif kind == "shift":
                    pe.wait_ge(*max_done.after(d, 16 * n + 16))
                    last = nc.tensor.transpose(ps[0:32, 0, 0:P], row_max[:, n, :], ident[:, :])
                elif kind == "k2":
                    pe.wait_ge(*ctx1_in.after(d, 16))
                    last = project(ps[:, 0, :], w1k_sb, slice(0, P), ctx_v)
                elif kind == "v2":
                    last = project_T(ps, ctx_v, w1v_sb, range(2 * n, 2 * n + 2))
                elif kind == "q2":
                    pe.wait_ge(*x1_made.after(d, 2))
                    last = project(ps[:, 0, :], w1q_sb, slice(0, P), x1)
                elif kind == "s2":
                    pe.wait_ge(*q2_made.after(d, 1))
                    pe.wait_ge(*k2_made.after(d, 1))
                    for j in range(2):
                        nb = 2 * n + j
                        last = nc.tensor.matmul(ps[:, j, :], q2[:, nb * P:nb * P + P], k2[:, :], start=True, stop=True)
                elif kind == "t2":
                    pe.wait_ge(*probs2_made.after(d, 2))
                    for j in range(2):
                        for nb in range(KB):
                            mb = 2 * n + j
                            last = nc.tensor.transpose(ps[:, j, nb * P:nb * P + P],
                                                       probs2[:, nb, mb * P:mb * P + P], ident[:, :])
                elif kind == "o2":
                    pe.wait_ge(*probs2T_made.after(d, 2))
                    pe.wait_ge(*v2_made.after(d, 2))
                    for mb in range(KB):
                        last = nc.tensor.matmul(ps[:, 0, :], values2[:, mb, n * P:n * P + P], probs2T[:, mb, :],
                                                start=(mb == 0), stop=(mb == KB - 1))
                last.then_inc(made[kind].sem, 1)

            def scores(b, p, t):
                sub, i = divmod(t, GROUP)
                head, kp = GROUP * (sub // 2) + i, sub % 2
                ps = claim(b, "st", 0, t)
                if t == 0:
                    pe.wait_ge(*shift_in[0].after(b, 16))
                if t == 16:
                    pe.wait_ge(*shift_in[1].after(b, 16))
                for j in range(2):
                    kb = 2 * kp + j
                    last = nc.tensor.matmul(ps[:, j, :], k_stack[p][0:ROWS, head, kb * P:kb * P + P],
                                            q_stack[p][0:ROWS, head, :], start=True, stop=True)
                last.then_inc(made["st"].sem, 1)

            def maxima(b, o, t):
                head, qp = divmod(t, 2)
                ps = claim(b, "mx", 1, t)
                if t == 0:
                    pe.wait_ge(*stack_in[0].after(b + 2, 0))
                    pe.wait_ge(*maskrow_in[0].after(b + 2, 0))
                if t == 16:
                    pe.wait_ge(*stack_in[1].after(b + 2, 0))
                    pe.wait_ge(*maskrow_in[1].after(b + 2, 0))
                for j in range(2):
                    qb = 2 * qp + j
                    last = nc.tensor.matmul(ps[:, j, :], q_stack[o][0:ROW_MAX, head, qb * P:qb * P + P],
                                            k_stack[o][0:ROW_MAX, head, :], start=True, stop=True)
                last.then_inc(made["mx"].sem, 1)

            def attend(d, p, sub, kb):
                g = sub // 2
                if kb % 2 == 0:
                    pe.wait_ge(*exp_done.after(d, GROUP * sub + GROUP))
                if kb == 0:
                    pe.wait_ge(*att_copied.after(d, g))
                    if g == 0:
                        pe.wait_ge(*v_squared.after(d, 2))
                for i in range(GROUP):
                    last = nc.tensor.matmul(att[32 * i:32 * i + 32, :], values[p][:, kb, GROUP * g + i, :],
                                            probs[sub % 2][:, i, kb % 2, :], start=(kb == 0), stop=(kb == KB - 1))
                if kb % 2 == 1:
                    last.then_inc(att_done.sem, 1)

            def denominators(d, g):
                pe.wait_ge(*sum_done.after(d, GROUP * g + GROUP))
                if g == 0:
                    pe.wait_ge(*den_copied.after(d, 0))
                for i in range(GROUP):
                    last = nc.tensor.matmul(den[32 * i:32 * i + 32, :], pick[:, g, :], pairs[1][:, i, :],
                                            start=(g == 0), stop=(g == HEADS // GROUP - 1))
                last.then_inc(den_done.sem, 1)

            def body(b, p):
                if b == FIRST + 1:
                    pe.wait_ge(wk_in, 32)
                if b == FIRST + 2:
                    pe.wait_ge(weights_in, WEIGHTS)
                    pe.wait_ge(consts, 4)
                    pe.wait_ge(ones_made, ONES)
                for t in range(STEPS):
                    sub, quad = t // GROUP - 1, t % GROUP
                    group = t // 8 - 1
                    if exists(b):
                        scores(b, p, t)
                    if exists(b + 1):
                        maxima(b, 1 - p, t)
                    if quad < 2:
                        if sub < 0 and exists(b - 1):
                            attend(b - 1, 1 - p, SUBS - 1, 2 + quad)
                        if sub >= 0 and exists(b):
                            attend(b, p, sub, 2 * (sub % 2) + quad)
                    if t % 8 == 3:
                        if group < 0 and exists(b - 1):
                            denominators(b - 1, HEADS // GROUP - 1)
                        if group >= 0 and exists(b):
                            denominators(b, group)
                    for kind, off, n in FILLERS[t]:
                        if exists(b + off):
                            filler(b, kind, off, n)

            iterations(pe, body)

        @block.scalar
        def _(act):

            def exp(b, t):
                sub, i = divmod(t, GROUP)
                if i == 0:
                    if b == 0 and t == 0:
                        act.wait_ge(maskrow_out, 16)
                    act.wait_ge(*att_done.after(b, sub - 1))
                    act.wait_ge(*pair_done.after(b, GROUP * (sub - 1)))
                act.wait_ge(*made["st"].after(b, t + 1))
                nc.scalar.activation(probs[sub % 2][:, i, :, :], slot("st", b, t), ACT.Exp, scale=SCALE)\
                    .then_inc(exp_done.sem, 1)

            def rows(dram, d):
                return dram[index(d)].rearrange("(c p) t -> p c t", p=P)

            def load_maskrow(d, p, half):
                if isinstance(d, int) and d == 0:
                    act.wait_ge(ones_made, ONES)
                    act.wait_ge(maskrow_out, 16)
                act.wait_ge(*made["st"].after(d - 2, 16 * half + 16))
                act.wait_ge(*maskrow_in[half].after(d, 0))
                act.dma_start(k_stack[p][ROW_MASK:ROW_MASK + 1, half * HALF:(half + 1) * HALF, :],
                              maskrow_dram[bass.ds(index(d), 1), half * HALF * T:(half + 1) * HALF * T]
                              .rearrange("o (h t) -> o h t", t=T)).then_inc(maskrow_in[half].sem, 16)

            def loads(b, p, t):
                for half in range(2):
                    when = AT[f"load maskrow {half}"]
                    d = due(b, t, when)
                    if d is not None:
                        load_maskrow(d, parity(p, when), half)
                d = due(b, t, AT["load x"])
                if d is not None:
                    if exists(d + 3):
                        act.wait_ge(*made["q"].after(d + 3, 2))
                    act.dma_start(xs[:, :, :], rows(x_in, d)).then_inc(xr_in.sem, 16)
                    act.dma_start(mask_b8[:, :], mask_in[index(d), :].partition_broadcast(P)).then_inc(mask_in_.sem, 16)
                d = due(b, t, AT["load k"])
                if d is not None and not (isinstance(d, int) and d == 0):
                    act.wait_ge(*made["k"].after(d - 1, 2))
                    act.dma_start(ctx_k[:, :, :], rows(ctx_in, d)).then_inc(ctxk_in.sem, 16)
                d = due(b, t, AT["load q"])
                if d is not None and not (isinstance(d, int) and d == 0):
                    act.wait_ge(*x_scaled.after(d - 4, 2))
                    act.dma_start(xs[:, :, :], rows(x_in, d)).then_inc(xq_in.sem, 16)
                d = due(b, t, AT["load ctx 1"])
                if d is not None:
                    if exists(d + 1):
                        act.wait_ge(*made["v"].after(d + 1, 1))
                    act.dma_start(ctx_v[:, :, :], rows(ctx_in, d)).then_inc(ctx1_in.sem, 16)
                d = due(b, t, AT["load v"])
                if d is not None:
                    if exists(d - 2):
                        act.wait_ge(*made["k2"].after(d - 2, 1))
                        act.wait_ge(*made["v2"].after(d - 2, 2))
                    act.dma_start(ctx_v[:, :, :], rows(ctx_in, d)).then_inc(ctxv_in.sem, 16)
                d = due(b, t, AT["result"])
                if d is not None:
                    act.wait_ge(*result_made.after(d, 2))
                    act.dma_start(rows(out, d), x1[:, :, :]).then_inc(result_out.sem, 16)

            def exp2(d, n):
                act.wait_ge(*max2_done.after(d, n + 1))
                if n == 0:
                    act.wait_ge(*var_made.after(d, 2))
                for nb in (2 * n, 2 * n + 1):
                    nc.scalar.activation(probs2[:, nb, :], slot("s2", d, n)[:, nb % 2, :], ACT.Exp,
                                         bias=stats2[:, 0, nb:nb + 1], accum_out=stats2[:, 1, nb:nb + 1])\
                        .then_inc(exp2_done.sem, 1)

            def transposed(d, n):
                act.wait_ge(*made["t2"].after(d, n + 1))
                if n == 0:
                    act.wait_ge(*made["o2"].after(d - 1, 2))
                nc.scalar.activation(probs2T[:, 2 * n:2 * n + 2, :], slot("t2", d, n), ACT.Copy)\
                    .then_inc(probs2T_made.sem, 1)

            def copy_moments(d, g):
                act.wait_ge(*att_done.after(d, 2 * g + 2))
                act.wait_ge(*moments_in[g % 2].after(d, 16 * 2 * GROUP * (g // 2)))
                nc.scalar.activation(raw[g % 2][:, :], att[:, :], ACT.Copy).then_inc(att_copied.sem, 1)

            def part_1(n, kind, d, half, bias):
                act.wait_ge(*made[kind].after(d, half + 1))
                if half == 0:
                    if n == 0:
                        act.wait_ge(*parts_out[1].after(d, 0))
                    else:
                        act.wait_ge(*parts_out[0].after(d, 32))
                nc.scalar.activation(split[:, half, 0, :], slot(kind, d, half)[:, 0, :], ACT.Identity,
                                     bias=bias[:, half:half + 1]).then_inc(part1[n].sem, 1)

            def part_2(n, d, half):
                act.wait_ge(*rest_made[n].after(d, half + 1))
                nc.scalar.activation(split[:, half, 1, :], rest[:, :], ACT.Copy).then_inc(part2[n].sem, 1)

            act.dma_start(xs[:, :, :], rows(x_in, 0)).then_inc(xq_in.sem, 16)
            act.dma_start(ctx_k[:, :, :], rows(ctx_in, 0)).then_inc(ctxk_in.sem, 16)
            act.wait_ge(wq_in, 32)
            act.wait_ge(wk_in, 32)

            def body(b, p):
                for t in range(STEPS):
                    if exists(b):
                        exp(b, t)
                    loads(b, p, t)
                    for g in range(HEADS // GROUP):
                        d = due(b, t, 8 * g + 10)
                        if d is not None:
                            copy_moments(d, g)
                    d = due(b, t, AT["copy den"])
                    if d is not None:
                        act.wait_ge(*den_done.after(d, SUBS // 2))
                        act.wait_ge(*den_out.after(d, 0))
                        nc.scalar.activation(den_rows[:, :], den[:, :], ACT.Copy).then_inc(den_copied.sem, 1)
                    for n, kind in enumerate("qk"):
                        for half in range(2):
                            d = due(b, t, AT[kind, half] + 1)
                            if d is not None:
                                part_2(n, d, half)
                    d = due(b, t, AT["scale 0"])
                    if d is not None:
                        act.wait_ge(*sum2_inv.after(d, 1))
                        for nb in range(2):
                            last = nc.scalar.activation(probs2[:, nb, :], probs2[:, nb, :], ACT.Copy,
                                                        scale=stats2[:, 2, nb:nb + 1])
                        last.then_inc(probs2_made.sem, 1)
                    d = due(b, t, AT["mask"])
                    if d is not None:
                        act.wait_ge(*mask_in_.after(d, 16))
                        nc.scalar.activation(mask_b[:, :], mask_b8[:, :], ACT.Copy, accum_out=stats[:, 0:1])\
                            .then_inc(mask_ready.sem, 1)
                    for half in range(2):
                        d = due(b, t, AT[f"x sums {half}"])
                        if d is not None:
                            act.wait_ge(*x_masked.after(d, half + 1))
                            nc.scalar.activation(xs[:, half, :], xs[:, half, :], ACT.Copy,
                                                 accum_out=stats[:, 2 + half:3 + half]).then_inc(x_sum.sem, 1)
                            if half == 0:
                                act.wait_ge(*made["t2"].after(d, 0))
                            act.wait_ge(*x_sum.after(d, half + 1))
                            nc.scalar.activation(square[:, half, :], xs[:, half, :], ACT.Square,
                                                 accum_out=stats[:, 4 + half:5 + half]).then_inc(x_sumsq.sem, 1)
                    d = due(b, t, AT["mean^2"])
                    if d is not None:
                        act.wait_ge(*mean_made.after(d, 2))
                        act.wait_ge(*x_sumsq.after(d, 2))
                        nc.scalar.activation(square[:, :, :], mean[:, :, :], ACT.Square).then_inc(mean_squared.sem, 1)
                    d = due(b, t, AT["sqrt"])
                    if d is not None:
                        act.wait_ge(*stat_steps.after(d, 5))
                        nc.scalar.activation(spread[:, :], stats[:, 10:12], ACT.Sqrt).then_inc(spread_done.sem, 1)
                        act.wait_ge(*var_clamped.after(d, 1))
                        nc.scalar.activation(ex2[:, :, :], ex2[:, :, :], ACT.Sqrt).then_inc(std_done.sem, 1)
                    for kind, off, n in FILLERS[t]:
                        if not exists(b + off):
                            continue
                        if kind == "s2":
                            exp2(b + off, n)
                        elif kind == "q":
                            part_1(0, kind, b + off, n, bq_sb)
                        elif kind == "k":
                            part_1(1, kind, b + off, n, bk_sb)
                        elif kind == "t2":
                            transposed(b + off, n)
                        elif kind == "k2":
                            act.wait_ge(*made["k2"].after(b + off, 1))
                            act.wait_ge(*made["s2"].after(b + off - 1, 2))
                            nc.scalar.activation(k2[:, :], slot("k2", b + off, 0)[:, 0, :], ACT.Identity, bias=b1k_sb[:, :])\
                                .then_inc(k2_hi.sem, 1)
                        elif kind == "q2":
                            act.wait_ge(*made["q2"].after(b + off, 1))
                            act.wait_ge(*made["s2"].after(b + off - 1, 2))
                            nc.scalar.activation(q2[:, :], slot("q2", b + off, 0)[:, 0, :], ACT.Identity, bias=b1q_sb[:, :])\
                                .then_inc(q2_hi.sem, 1)

            iterations(act, body)
            act.wait_ge(*result_out.after(B, 0))

        @block.gpsimd
        def _(pool):
            nc.gpsimd.memset(ident[:, :], 0.0).then_inc(consts, 1)
            pool.wait_ge(consts, 1)
            nc.gpsimd.affine_select(out=ident[:, :], in_=ident[:, :], compare_op=ALU.not_equal, fill=1.0, base=0,
                                    pattern=[[-1, P]], channel_multiplier=1).then_inc(consts, 1)
            for n, stack in enumerate(q_stack):
                pool.wait_ge(consts, 2 + n)
                nc.gpsimd.memset(stack[ROW_MASK:P, :, :].bitcast(fp32), TWO_BF16_ONES).then_inc(consts, 1)

            def part_3(n, d, half):
                pool.wait_ge(*part2[n].after(d, half + 1))
                nc.gpsimd.tensor_tensor(out=split[:, half, 2, :], in0=rest[:, :], in1=split[:, half, 1, :],
                                        op=ALU.subtract).then_inc(part3[n].sem, 1)

            def pair(b, t):
                sub, i = divmod(t, GROUP)
                if t % 8 == 0:
                    pool.wait_ge(*sum_done.after(b, GROUP * (t // 8)))
                if t % 8 == 4:
                    pool.wait_ge(*den_done.after(b, t // 8))
                pool.wait_ge(*exp_done.after(b, t + 1))
                nc.gpsimd.tensor_tensor(out=pairs[sub % 2][:, i, :], in0=probs[sub % 2][:, i, 0, :],
                                        in1=probs[sub % 2][:, i, 1, :], op=ALU.add).then_inc(pair_done.sem, 1)

            def body(b, p):
                for t in range(STEPS):
                    if exists(b):
                        pair(b, t)
                    for n, kind in enumerate("qk"):
                        for half in range(2):
                            d = due(b, t, AT[kind, half] + 2)
                            if d is not None:
                                part_3(n, d, half)
                    for half in range(2):
                        when = AT[f"v^2 {half}"]
                        d = due(b, t, when)
                        if d is not None:
                            pool.wait_ge(*v_biased.after(d, 1))
                            cols = slice(HEADS * 2 * half, HEADS * 2 * half + HEADS * 2)
                            v = values[parity(p, when)][:, :, :, :].rearrange("p k h e -> p (k h) e")
                            nc.gpsimd.tensor_tensor(out=v[:, cols, D:2 * D], in0=v[:, cols, 0:D], in1=v[:, cols, 0:D],
                                                    op=ALU.mult).then_inc(v_squared.sem, 1)
                        d = due(b, t, AT[f"mask x {half}"])
                        if d is not None:
                            pool.wait_ge(*mask_ready.after(d, 1))
                            pool.wait_ge(*xr_in.after(d, 16))
                            nc.gpsimd.tensor_tensor(out=xs[:, half, :], in0=xs[:, half, :], in1=mask_b[:, :],
                                                    op=ALU.mult).then_inc(x_masked.sem, 1)
                        d = due(b, t, AT[f"mean {half}"])
                        if d is not None:
                            pool.wait_ge(*moments_in[0].after(d + 1, 0))
                            pool.wait_ge(*moments_in[1].after(d + 1, 0))
                            pool.wait_ge(*inv_in.after(d, 16 * CH))
                            nc.gpsimd.tensor_tensor(out=mean[:, half, :], in0=mean[:, half, :], in1=inv_den[:, half, :],
                                                    op=ALU.mult).then_inc(mean_made.sem, 1)
                        d = due(b, t, AT[f"var {half}"])
                        if d is not None:
                            pool.wait_ge(*mean_squared.after(d, 1))
                            pool.wait_ge(*ex2_made.after(d, 2))
                            nc.gpsimd.tensor_tensor(out=ex2[:, half, :], in0=ex2[:, half, :], in1=square[:, half, :],
                                                    op=ALU.subtract).then_inc(var_made.sem, 1)
                    d = due(b, t, AT["x mask"])
                    if d is not None:
                        pool.wait_ge(*x_shifted.after(d, 1))
                        nc.gpsimd.tensor_tensor(out=x1[:, 0, :], in0=x1[:, 0, :], in1=mask_b[:, :],
                                                op=ALU.mult).then_inc(x1_made.sem, 1)

            pool.wait_ge(consts, 4)
            iterations(pool, body)

        @block.vector
        def _(dve):
            nc.vector.memset(pick[:, :, :], 0.0).then_inc(pick_cleared, 1)
            dve.wait_ge(pick_cleared, 1)
            for g in range(SUBS // 2):
                nc.vector.memset(pick[:, g, :].rearrange("p (k j) -> p j k", j=SUBS // 2)[:, g, :], 1.0)\
                    .then_inc(ones_made, 1)
            for stack in k_stack:
                nc.vector.memset(stack[ROW_MASK:P, :, :].bitcast(fp32), TWO_BF16_ONES).then_inc(ones_made, 1)
            dve.wait_ge(mask_u8_in, 16)
            nc.vector.tensor_scalar(mask_f, mask_u8[:, :], 1.0, MASKED, ALU.subtract, ALU.mult)\
                .then_inc(mask_scaled, 1)
            dve.wait_ge(mask_scaled, 1)
            for h in range(HEADS):
                nc.vector.tensor_copy(maskrow[:, h * T:h * T + T], mask_f).then_inc(maskrow_made, 1)
            dve.wait_ge(wq_in, 32)
            dve.wait_ge(wk_in, 32)
            dve.wait_ge(weights_in, WEIGHTS)

            def part_rest(n, kind, d, half, bias):
                dve.wait_ge(*part1[n].after(d, half + 1))
                if half == 1:
                    dve.wait_ge(*part3[n].after(d, 1))
                elif n == 0:
                    dve.wait_ge(*part3[1].after(d, 0))
                else:
                    dve.wait_ge(*part3[0].after(d, 2))
                nc.vector.scalar_tensor_tensor(out=rest[:, :], in0=slot(kind, d, half)[:, 0, :],
                                               scalar=bias[:, half:half + 1], in1=split[:, half, 0, :],
                                               op0=ALU.add, op1=ALU.subtract).then_inc(rest_made[n].sem, 1)

            def add_value_bias(d, dst):
                dve.wait_ge(*made["v"].after(d, 1))
                ps = slot("v", d, 0)
                for kb in range(KB):
                    last = nc.vector.tensor_tensor(
                        out=dst[:, kb, :, 0:D],
                        in0=ps[:, kb // 2, (kb % 2) * C:(kb % 2) * C + C].rearrange("p (h d) -> p h d", d=D),
                        in1=bv_sb[:, :].rearrange("p (h d) -> p h d", d=D), op=ALU.add)
                last.then_inc(v_biased.sem, 1)

            def add_value2_bias(d, n):
                dve.wait_ge(*made["v2"].after(d, n + 1))
                if n == 0:
                    dve.wait_ge(*made["o2"].after(d - 1, 2))
                nc.vector.tensor_tensor(out=values2[:, 2 * n:2 * n + 2, :],
                                        in0=slot("v2", d, n)[:, 0, :].rearrange("p (k c) -> p k c", k=2),
                                        in1=b1v_sb[:, :].unsqueeze(1).to_broadcast([P, 2, C]),
                                        op=ALU.add).then_inc(v2_made.sem, 1)

            def shift_rows(d, half):
                ps = slot("shift", d, half)[0:32, 0, 0:P]
                dve.wait_ge(*made["shift"].after(d, half + 1))
                dve.wait_ge(*shift_out[1 - half].after(d + half - 1, 16))
                nc.vector.tensor_scalar(neg_max[:, 0, :], ps, -1.0, None, ALU.mult).then_inc(neg1.sem, 1)
                dve.wait_ge(*neg1.after(d, half + 1))
                nc.vector.scalar_tensor_tensor(out=neg_rest[:, :], in0=ps, scalar=-1.0, in1=neg_max[:, 0, :],
                                               op0=ALU.mult, op1=ALU.subtract).then_inc(shift_rest.sem, 1)
                dve.wait_ge(*shift_rest.after(d, half + 1))
                nc.vector.tensor_copy(neg_max[:, 1, :], neg_rest[:, :]).then_inc(neg2.sem, 1)
                dve.wait_ge(*neg2.after(d, half + 1))
                nc.vector.tensor_tensor(out=neg_max[:, 2, :], in0=neg_rest[:, :], in1=neg_max[:, 1, :],
                                        op=ALU.subtract).then_inc(neg3.sem, 1)

            def sum_pairs(d, n):
                g, i = divmod(n, GROUP)
                dve.wait_ge(*pair_done.after(d, 8 * g + 4 + i + 1))
                nc.vector.tensor_tensor(out=pairs[1][:, i, :], in0=pairs[0][:, i, :], in1=pairs[1][:, i, :],
                                        op=ALU.add).then_inc(sum_done.sem, 1)

            def instance_stats(d):
                s = stats
                dve.wait_ge(*mask_ready.after(d, 1))
                nc.vector.reciprocal(s[:, 1:2], s[:, 0:1]).then_inc(stat_steps.sem, 1)
                dve.wait_ge(*stat_steps.after(d, 1))
                dve.wait_ge(*x_sum.after(d, 2))
                nc.vector.tensor_scalar(s[:, 6:8], s[:, 2:4], s[:, 1:2], None, ALU.mult).then_inc(stat_steps.sem, 1)
                dve.wait_ge(*x_sumsq.after(d, 2))
                dve.wait_ge(*stat_steps.after(d, 2))
                nc.vector.tensor_tensor(out=s[:, 8:10], in0=s[:, 6:8], in1=s[:, 6:8], op=ALU.mult)\
                    .then_inc(stat_steps.sem, 1)
                dve.wait_ge(*stat_steps.after(d, 3))
                nc.vector.scalar_tensor_tensor(out=s[:, 10:12], in0=s[:, 4:6], scalar=s[:, 1:2], in1=s[:, 8:10],
                                               op0=ALU.mult, op1=ALU.subtract).then_inc(stat_steps.sem, 1)
                dve.wait_ge(*stat_steps.after(d, 4))
                nc.vector.tensor_scalar(s[:, 10:12], s[:, 10:12], 0.0, EPS, ALU.max, ALU.add)\
                    .then_inc(stat_steps.sem, 1)

            def split_q2(d):
                ps = slot("q2", d, 0)[:, 0, :]
                dve.wait_ge(*q2_hi.after(d, 1))
                nc.vector.scalar_tensor_tensor(out=q2[64:128, :], in0=ps[64:128], scalar=b1q_sb[64:128, :],
                                               in1=q2[64:128, :].bitcast(fp32), op0=ALU.add, op1=ALU.subtract)\
                    .then_inc(q2_made.sem, 1)

            def split_k2(d):
                ps = slot("k2", d, 0)[:, 0, :]
                dve.wait_ge(*k2_hi.after(d, 1))
                for lo in (32, 96):
                    last = nc.vector.scalar_tensor_tensor(
                        out=k2[lo:lo + 32, :], in0=ps[lo:lo + 32], scalar=b1k_sb[lo:lo + 32, :],
                        in1=k2[lo:lo + 32, :].bitcast(fp32), op0=ALU.add, op1=ALU.subtract)
                last.then_inc(k2_made.sem, 1)

            def body(b, p):
                for t in range(STEPS):
                    if exists(b + 1):
                        dve.wait_ge(*made["mx"].after(b + 1, t + 1))
                        if t % 16 == 0:
                            dve.wait_ge(*made["shift"].after(b, t // 16 + 1))
                        nc.vector.reduce_max(row_max[:, t // 16, 2 * (t % 16):2 * (t % 16) + 2], slot("mx", b + 1, t),
                                             axis=AX.X).then_inc(max_done.sem, 1)
                    for n in range(2):
                        d = due(b, t, AT["s2", n])
                        if d is not None:
                            dve.wait_ge(*made["s2"].after(d, n + 1))
                            nc.vector.reduce_max(stats2[:, 0, 2 * n:2 * n + 2], slot("s2", d, n), axis=AX.X,
                                                 negate=True).then_inc(max2_done.sem, 1)
                    for n in range(HEADS):
                        d = due(b, t, GROUP * (2 * (n // GROUP) + 1) + n % GROUP + SUM_LAG)
                        if d is not None:
                            sum_pairs(d, n)
                    d = due(b, t, AT["invert"])
                    if d is not None:
                        dve.wait_ge(*den_in.after(d, 16))
                        nc.vector.reciprocal(dens[:, :], dens[:, :]).then_inc(inv_made.sem, 1)
                    d = due(b, t, AT["ex2"])
                    if d is not None:
                        dve.wait_ge(*moments_in[0].after(d + 1, 0))
                        dve.wait_ge(*moments_in[1].after(d + 1, 0))
                        dve.wait_ge(*inv_in.after(d, 16 * CH))
                        for half in range(CH):
                            nc.vector.tensor_tensor(out=ex2[:, half, :], in0=ex2[:, half, :], in1=inv_den[:, half, :],
                                                    op=ALU.mult).then_inc(ex2_made.sem, 1)
                    d = due(b, t, AT["stats"])
                    if d is not None:
                        instance_stats(d)
                    d = due(b, t, AT["clamp"])
                    if d is not None:
                        dve.wait_ge(*var_made.after(d, 2))
                        nc.vector.tensor_scalar(ex2[:, :, :], ex2[:, :, :], 0.0, None, ALU.max)\
                            .then_inc(var_clamped.sem, 1)
                    d = due(b, t, AT["x scale"])
                    if d is not None:
                        dve.wait_ge(*spread_done.after(d, 1))
                        nc.vector.reciprocal(stats[:, 12:14], spread[:, :]).then_inc(stat_steps.sem, 1)
                        dve.wait_ge(*std_done.after(d, 1))
                        dve.wait_ge(*result_out.after(d, 0))
                        for half in range(CH):
                            nc.vector.scalar_tensor_tensor(out=x1[:, half, :], in0=xs[:, half, :],
                                                           scalar=stats[:, 6 + half:7 + half], in1=ex2[:, half, :],
                                                           op0=ALU.subtract, op1=ALU.mult).then_inc(x_scaled.sem, 1)
                    d = due(b, t, AT["x shift"])
                    if d is not None:
                        dve.wait_ge(*stat_steps.after(d, 6))
                        for half in range(CH):
                            dve.wait_ge(*x_scaled.after(d, half + 1))
                            nc.vector.scalar_tensor_tensor(out=x1[:, half, :], in0=x1[:, half, :],
                                                           scalar=stats[:, 12 + half:13 + half], in1=mean[:, half, :],
                                                           op0=ALU.mult, op1=ALU.add).then_inc(x_shifted.sem, 1)
                    d = due(b, t, AT["x mask"])
                    if d is not None:
                        dve.wait_ge(*x_shifted.after(d, 2))
                        nc.vector.tensor_tensor(out=x1[:, 1, :], in0=x1[:, 1, :], in1=mask_b[:, :],
                                                op=ALU.mult).then_inc(x1_made.sem, 1)
                    d = due(b, t, AT["scale 1"])
                    if d is not None:
                        dve.wait_ge(*exp2_done.after(d, KB))
                        nc.vector.reciprocal(stats2[:, 2, :], stats2[:, 1, :]).then_inc(sum2_inv.sem, 1)
                        dve.wait_ge(*sum2_inv.after(d, 1))
                        for nb in range(2, KB):
                            last = nc.vector.tensor_scalar(probs2[:, nb, :], probs2[:, nb, :], stats2[:, 2, nb:nb + 1],
                                                           None, ALU.mult)
                        last.then_inc(probs2_made.sem, 1)
                    for kind, off, n in FILLERS[t]:
                        d = b + off
                        if not exists(d):
                            continue
                        if kind == "q":
                            part_rest(0, kind, d, n, bq_sb)
                        elif kind == "k":
                            part_rest(1, kind, d, n, bk_sb)
                        elif kind == "v":
                            dve.wait_ge(*att_done.after(d - 2, SUBS))
                            add_value_bias(d, values[(p + off) % 2])
                        elif kind == "shift":
                            shift_rows(d, n)
                        elif kind == "k2":
                            split_k2(d)
                        elif kind == "v2":
                            add_value2_bias(d, n)
                        elif kind == "q2":
                            split_q2(d)
                        elif kind == "o2":
                            dve.wait_ge(*made["o2"].after(d, n + 1))
                            nc.vector.tensor_tensor(out=x1[:, n, :], in0=slot("o2", d, n)[:, 0, :], in1=x1[:, n, :],
                                                    op=ALU.add).then_inc(result_made.sem, 1)

            iterations(dve, body)


def kernel(x, ctx_2048, mask_Bx1x2048_bf1, L0_xattn_Wq, L0_xattn_bq, L0_xattn_Wk, L0_xattn_bk, L0_xattn_Wv,
           L0_xattn_bv, L1_xattn_Wq, L1_xattn_bq, L1_xattn_Wk, L1_xattn_bk, L1_xattn_Wv, L1_xattn_bv):
    import numpy as np
    import concourse.bacc as bacc
    from concourse import mybir
    from concourse.bass_utils import run_bass_kernel_spmd

    def T_(w):
        return np.ascontiguousarray(np.asarray(w).T)

    def halves(v):
        return np.ascontiguousarray(np.asarray(v).reshape(2, 128).T)

    arrays = dict(
        x=np.ascontiguousarray(x), ctx=np.ascontiguousarray(ctx_2048),
        mask=np.ascontiguousarray(mask_Bx1x2048_bf1).reshape(16, 512).view(np.uint8),
        wqT=T_(L0_xattn_Wq), bq=halves(L0_xattn_bq), wkT=T_(L0_xattn_Wk), bk=halves(L0_xattn_bk),
        wvT=T_(L0_xattn_Wv), bv=np.ascontiguousarray(L0_xattn_bv),
        w1qT=np.tile(T_(L1_xattn_Wq), (1, 4)), b1q=np.tile(np.asarray(L1_xattn_bq), 4).reshape(128, 1),
        w1kT=np.tile(T_(L1_xattn_Wk), (1, 4)), b1k=np.tile(np.asarray(L1_xattn_bk), 4).reshape(128, 1),
        w1vT=T_(L1_xattn_Wv), b1v=np.ascontiguousarray(L1_xattn_bv))
    nc = bacc.Bacc("TRN2", target_bir_lowering=False, num_devices=1)
    args = [nc.dram_tensor(f"{n}_dram", a.shape, mybir.dt.from_np(a.dtype), kind="ExternalInput").ap()
            for n, a in arrays.items()]
    out = nc.dram_tensor("out_dram", (16, 256, 512), mybir.dt.float32, kind="ExternalOutput").ap()
    build(nc, *args, out)
    r = run_bass_kernel_spmd(nc, [{f"{n}_dram": a for n, a in arrays.items()}], core_ids=[0])
    return r.results[0]["out_dram"]
```
